# Optimizing a Trainium2 kernel written in Bass

```python
import numpy as np
import jax
import jax.numpy as jnp

def _softmax(x, axis=-1):
    return jax.nn.softmax(x, axis=axis)

def _gelu(x):
    return jax.nn.gelu(x, approximate=True)

def _silu(x):
    return jax.nn.silu(x)

def _sigmoid(x):
    return jax.nn.sigmoid(x)

def _layernorm(x, axis=-1, eps=1e-05):
    m = jnp.mean(x, axis=axis, keepdims=True)
    v = jnp.var(x, axis=axis, keepdims=True)
    return (x - m) / jnp.sqrt(v + eps)

def _scatter_add(tgt, idx, src, axis=0):
    return tgt.at[idx].add(src)

def _segment_sum(src, seg, n):
    return jax.ops.segment_sum(src, seg, n)
kernel_name = 'mk_gnn_ffn_d1_gnn_r16_8a17b1'

def setup_inputs(seed: int=0):
    np.random.seed(seed)
    _w = jnp.asarray

    def _rec_inputs():
        import jax
        import jax.numpy as jnp
        _gk = jax.random.key(seed)
        x = -0.0003713 + 1 * jax.random.normal(jax.random.fold_in(_gk, 1), (6250, 256), jnp.float32)
        src = jax.random.randint(jax.random.fold_in(_gk, 2), (100000,), 0, 6250, jnp.int32)
        dst = jax.random.randint(jax.random.fold_in(_gk, 3), (100000,), 0, 6250, jnp.int32)
        _o = jnp.argsort(dst, stable=True)
        src = src[_o]
        dst = dst[_o]
        return (x, src, dst)
    x, src, dst = _rec_inputs()

    def _L0_gnn_setup():
        import jax, jax.numpy as jnp
        import numpy as np
        N_NODES = 3125
        N_EDGES = 20000
        IN_DIM = 256
        HID = 256
        N_LAYERS = 4
        EPS = 1e-05
        key = jax.random.key(seed)
        ks = jax.random.split(key, 12)
        s = 0.05
        x = jax.random.normal(ks[0], (N_NODES, IN_DIM), jnp.float32)
        rows = jax.random.randint(ks[1], (N_EDGES,), 0, N_NODES, dtype=jnp.int32)
        cols = jax.random.randint(ks[2], (N_EDGES,), 0, N_NODES, dtype=jnp.int32)
        W_in = jax.random.normal(ks[3], (IN_DIM, HID), jnp.float32) * s
        b_in = jnp.zeros((HID,), jnp.float32)
        Wl = jax.random.normal(ks[4], (N_LAYERS, HID, HID), jnp.float32) * s
        bl = jnp.zeros((N_LAYERS, HID), jnp.float32)
        Wg = jax.random.normal(ks[5], (N_LAYERS, HID, HID), jnp.float32) * s
        bg = jnp.zeros((N_LAYERS, HID), jnp.float32)
        gamma = jnp.ones((N_LAYERS, HID), jnp.float32)
        beta = jnp.zeros((N_LAYERS, HID), jnp.float32)
        return {'x': x, 'rows': rows, 'cols': cols, 'W_in': W_in, 'b_in': b_in, 'Wl': Wl, 'bl': bl, 'Wg': Wg, 'bg': bg, 'gamma': gamma, 'beta': beta}
    _L0_gnn_all = _L0_gnn_setup()
    _L0_gnn_in = {k: v for k, v in _L0_gnn_all.items() if k in ('W_in', 'b_in', 'Wl', 'bl', 'Wg', 'bg', 'gamma', 'beta')}
    del _L0_gnn_all

    def _L0_ffn_setup():
        import math
        import jax, jax.numpy as jnp
        import numpy as np
        CAPACITY_FACTOR = 1.25
        TOP_K = 2
        LN_EPS = 1e-05

        def _layer_norm(x, gamma, beta):
            mu = jnp.mean(x, axis=-1, keepdims=True)
            var = jnp.var(x, axis=-1, keepdims=True)
            return (x - mu) * jax.lax.rsqrt(var + LN_EPS) * gamma + beta
        key = jax.random.key(seed)
        ks = jax.random.split(key, 4)
        B, S, D, F, E = (8, 256, 256, 512, 8)
        x = jax.random.normal(ks[0], (B, S, D), dtype=jnp.float32)
        Wr = jax.random.normal(ks[1], (D, E), dtype=jnp.float32) / np.sqrt(D)
        br = jnp.zeros((E,), jnp.float32)
        W1 = jax.random.normal(ks[2], (E, D, F), dtype=jnp.float32) / np.sqrt(D)
        b1 = jnp.zeros((E, F), jnp.float32)
        W2 = jax.random.normal(ks[3], (E, F, D), dtype=jnp.float32) / np.sqrt(F)
        b2 = jnp.zeros((E, D), jnp.float32)
        gamma = jnp.ones((D,), jnp.float32)
        beta = jnp.zeros((D,), jnp.float32)
        return {'x': x, 'Wr': Wr, 'br': br, 'W1': W1, 'b1': b1, 'W2': W2, 'b2': b2, 'gamma': gamma, 'beta': beta}
    _L0_ffn_all = _L0_ffn_setup()
    _L0_ffn_in = {k: v for k, v in _L0_ffn_all.items() if k in ('Wr', 'br', 'W1', 'b1', 'W2', 'b2', 'gamma', 'beta')}
    del _L0_ffn_all
    return {'x': x, 'src': src, 'dst': dst, 'L0_gnn_W_in': _L0_gnn_in['W_in'], 'L0_gnn_b_in': _L0_gnn_in['b_in'], 'L0_gnn_Wl': _L0_gnn_in['Wl'], 'L0_gnn_bl': _L0_gnn_in['bl'], 'L0_gnn_Wg': _L0_gnn_in['Wg'], 'L0_gnn_bg': _L0_gnn_in['bg'], 'L0_gnn_gamma': _L0_gnn_in['gamma'], 'L0_gnn_beta': _L0_gnn_in['beta'], 'L0_ffn_Wr': _L0_ffn_in['Wr'], 'L0_ffn_br': _L0_ffn_in['br'], 'L0_ffn_W1': _L0_ffn_in['W1'], 'L0_ffn_b1': _L0_ffn_in['b1'], 'L0_ffn_W2': _L0_ffn_in['W2'], 'L0_ffn_b2': _L0_ffn_in['b2'], 'L0_ffn_gamma': _L0_ffn_in['gamma'], 'L0_ffn_beta': _L0_ffn_in['beta']}

def reference(x, src, dst, L0_gnn_W_in, L0_gnn_b_in, L0_gnn_Wl, L0_gnn_bl, L0_gnn_Wg, L0_gnn_bg, L0_gnn_gamma, L0_gnn_beta, L0_ffn_Wr, L0_ffn_br, L0_ffn_W1, L0_ffn_b1, L0_ffn_W2, L0_ffn_b2, L0_ffn_gamma, L0_ffn_beta):
    import jax
    import jax.numpy as jnp

    def _L0_gnn_ref(x, rows, cols, W_in, b_in, Wl, bl, Wg, bg, gamma, beta):
        import jax, jax.numpy as jnp
        import numpy as np
        N_NODES = 3125
        N_EDGES = 20000
        IN_DIM = 256
        HID = 256
        N_LAYERS = 4
        EPS = 1e-05
        n = x.shape[0]
        deg = jax.ops.segment_sum(jnp.ones(rows.shape, x.dtype), rows, num_segments=n) + 1.0
        dinv = jax.lax.rsqrt(deg)[:, None]
        h = x @ W_in + b_in
        for l in range(Wl.shape[0]):
            h_scaled = h * dinv
            msg = jax.ops.segment_sum(h_scaled[cols], rows, num_segments=n) * dinv
            global_ctx = jnp.mean(h, axis=0) @ Wg[l] + bg[l]
            z = jax.nn.relu((h + msg) @ Wl[l] + bl[l] + global_ctx)
            mu = jnp.mean(z, axis=-1, keepdims=True)
            var = jnp.var(z, axis=-1, keepdims=True)
            h = (z - mu) * jax.lax.rsqrt(var + EPS) * gamma[l] + beta[l]
        return h

    def _L0_ffn_ref(x, Wr, br, W1, b1, W2, b2, gamma, beta):
        import math
        import jax, jax.numpy as jnp
        import numpy as np
        CAPACITY_FACTOR = 1.25
        TOP_K = 2
        LN_EPS = 1e-05

        def _layer_norm(x, gamma, beta):
            mu = jnp.mean(x, axis=-1, keepdims=True)
            var = jnp.var(x, axis=-1, keepdims=True)
            return (x - mu) * jax.lax.rsqrt(var + LN_EPS) * gamma + beta
        B, S, D = x.shape
        E = Wr.shape[1]
        N = B * S
        K = TOP_K
        logits = jnp.mean(x, axis=1) @ Wr + br
        routing_weights = jax.nn.softmax(logits, axis=-1)
        capacity = float(math.ceil(N * CAPACITY_FACTOR / E))
        expected_loads = routing_weights.sum(axis=0) * (N / B)
        scale = jnp.where(expected_loads > capacity, capacity / expected_loads, 1.0)
        routing_weights = jax.nn.softmax(routing_weights * scale, axis=-1)
        rw_tok = jnp.broadcast_to(routing_weights[:, None, :], (B, S, E)).reshape(N, E)
        top_w, top_i = jax.lax.top_k(rw_tok, K)
        top_w = jax.nn.softmax(top_w, axis=-1)
        xf = x.reshape(N, D)
        h = jax.nn.gelu(jnp.einsum('nd,edf->enf', xf, W1) + b1[:, None, :], approximate=False)
        y = jnp.einsum('enf,efd->end', h, W2) + b2[:, None, :]
        w_dense = jnp.zeros((N, E), x.dtype).at[jnp.arange(N)[:, None], top_i].add(top_w)
        out = jnp.einsum('ne,end->nd', w_dense, y).reshape(B, S, D)
        out = _layer_norm(out + x, gamma, beta)
        return out
    x = x + _L0_gnn_ref(_layernorm(x, axis=-1), src, dst, L0_gnn_W_in, L0_gnn_b_in, L0_gnn_Wl, L0_gnn_bl, L0_gnn_Wg, L0_gnn_bg, L0_gnn_gamma, L0_gnn_beta)
    x = x + _L0_ffn_ref(_layernorm(x, axis=-1)[None], L0_ffn_Wr, L0_ffn_br, L0_ffn_W1, L0_ffn_b1, L0_ffn_W2, L0_ffn_b2, L0_ffn_gamma, L0_ffn_beta)[0]
    return x

_drawn_inputs = setup_inputs


def setup_inputs(seed=0):
    import zlib

    import numpy as np

    out = dict(_drawn_inputs(seed))
    spreads = {'L0_gnn_b_in': (0.0, 0.1),
     'L0_gnn_bl': (0.0, 0.1),
     'L0_gnn_bg': (0.0, 0.1),
     'L0_gnn_gamma': (1.0, 0.2),
     'L0_gnn_beta': (0.0, 0.1),
     'L0_ffn_br': (0.0, 0.1),
     'L0_ffn_b1': (0.0, 0.436),
     'L0_ffn_b2': (0.0, 0.288),
     'L0_ffn_gamma': (1.0, 0.2),
     'L0_ffn_beta': (0.0, 0.1)}
    factors = {}
    for name, (base, spread) in spreads.items():
        noise = np.random.default_rng([zlib.crc32(name.encode()), seed]).standard_normal(out[name].shape)
        drawn = base * np.exp(spread * noise) if base else spread * noise
        out[name] = jnp.asarray(drawn.astype(out[name].dtype))
    for name, factor in factors.items():
        out[name] = (out[name] * factor).astype(out[name].dtype)
    return out
```

```python
import concourse.bass as bass
from concourse import mybir
from contextlib import ExitStack

F32 = mybir.dt.float32
F16 = mybir.dt.float16
BF16 = mybir.dt.bfloat16
F8 = mybir.dt.float8e4
I32 = mybir.dt.int32
I16 = mybir.dt.int16
U32 = mybir.dt.uint32
U16 = mybir.dt.uint16
U8 = mybir.dt.uint8
ALU = mybir.AluOpType
ACT = mybir.ActivationFunctionType
AX = mybir.AxisListType.X
ds = bass.ds

P = 128
N = 6250
NE = 100000
D = 256
KC = D // P
T = -(-N // P)
LAST = N - (T - 1) * P
NB = -(-NE // P)
CH = -(-NB // P)
WIN = 19
COLS = -(-NB // WIN) * WIN
PK = 5
FIELDS = -(-T // PK)
W = PK * P
HALF = W // 2
MG = 4
MLOOP = (T - 1) // (2 * MG)
PLANES = 3
RING = 3
LOOP = (T - 1) // RING
LAYERS = 4
EX, FF, TOP = 8, 512, 2
FC = FF // P
PADDST = (T + 1) * P - P // 2 + 8
EPS = 1e-5
SPAN = 30000.0
ROWNORM = 16.0
CAPACITY = float(-(-N * 5 // (4 * EX)))
ACT_FIELDS = (0, 4, 8, 1, 5, 9, 2, 3)
POOL_FIELDS = (6, 7)
DIV = -(-1024 // PK)
CONSTS = 11
SUP = RING
BEFORE_T, BEFORE_MM = 12, 22


def hold(eng, sem, value):
    eng.wait_ge(sem, value)
    eng.nop(nofuse=True)


class Steps:

    def __init__(self, eng, sem):
        self.eng, self.sem, self.base, self.k = eng, sem, 0, 0

    def at(self, base):
        self.base, self.k = base, 0

    def done(self, ins):
        ins.then_inc(self.sem, 1)
        self.k += 1

    def wait(self):
        self.eng.wait_ge(self.sem, self.base + self.k)

    def hold(self):
        hold(self.eng, self.sem, self.base + self.k)


def build(nc, x, src, dst, W_in, b_in, Wl, bl, Wg, bg, gamma, beta, Wr, br, W1, b1, W2, b2, fgamma, fbeta, out):
    assert RING * LOOP == T - 1 and 2 * MG * MLOOP == T - 1 and NB <= 2 * 512 and FIELDS <= 10
    A = nc.dram_tensor("adjacency", [T, P, T, P // 4], I32).ap()
    AG = nc.dram_tensor("adjacency_general", [FIELDS * PK, PLANES, P, T, P], BF16).ap()
    ctx = ExitStack()
    with ctx:
        def sb(name, shape, dt=F32):
            return ctx.enter_context(nc.sbuf_tensor(name, shape, dt))

        def sem(name):
            return ctx.enter_context(nc.semaphore(name))

        tab = sb("tab", [P, 2 * T, 2 * D], F16)
        tabf = tab[:, :, :].rearrange("p t f -> p (t f)").bitcast(F32)
        H = tabf[:, 0:T * D].rearrange("p (t f) -> p t f", f=D)
        spare = tabf[:, T * D:]
        stage = [spare[:, h * T * P:(h + 1) * T * P].bitcast(F8).rearrange("p (t m s) -> p t m s", m=MG, s=P)
                 for h in range(2)]
        stage32 = [spare[:, h * T * P:(h + 1) * T * P].bitcast(I32).rearrange("p (t m s) -> p t m s", m=MG, s=P // 4)
                   for h in range(2)]
        gstage = spare[:, 0:PLANES * W // 2].bitcast(BF16).rearrange("p (k s) -> p k s", s=W)
        at = [0]

        def part(region, words, size):
            at[0] += words
            assert at[0] <= size
            return region[:, at[0] - words:at[0]]

        def scratch(words):
            return part(spare, words, T * D)
        raw_src = scratch(CH * P).bitcast(I32).rearrange("p (k e) -> p k e", e=P)
        raw_dst = scratch(CH * P).bitcast(I32).rearrange("p (k e) -> p k e", e=P)
        rawf = scratch(CH * P).rearrange("p (k e) -> p k e", e=P)
        src_int = scratch(COLS).bitcast(I32)
        part_int = scratch(COLS).bitcast(I32)
        field = scratch(COLS).bitcast(I32)
        block_max = scratch(CH)
        before = scratch(T)
        at[0] = 0
        W1_s = scratch(TOP * KC * FF).rearrange("p (k f) -> p k f", f=FF)
        W2_s = scratch(TOP * FC * D).rearrange("p (a c f) -> p a c f", a=TOP, c=FC)
        SUPW = SUP * P
        gT = scratch(TOP * FC * SUPW).rearrange("p (f n) -> p f n", f=TOP * FC)
        xfT = scratch(KC * SUPW).rearrange("p (k n) -> p k n", k=KC)
        dstf = sb("dstf", [P, COLS])
        srcf = sb("srcf", [P, COLS])
        src_col = sb("src_col", [P, COLS])
        src_w = sb("src_w", [P, COLS])
        starts = sb("starts", [1, T], I32)
        RW = 12160
        region = sb("region", [P, RW])
        at[0] = 0

        def work(*shape):
            words = 1
            for k in shape:
                words *= k
            return part(region, words, RW)
        hot_s = work(WIN * W // 2).bitcast(BF16).rearrange("p (j s) -> p j s", s=W)
        hot_d = work(WIN * P // 2).bitcast(BF16).rearrange("p (j s) -> p j s", s=P)
        words = work(2 * W).bitcast(I32).rearrange("p (a s) -> p a s", s=W)
        masked = work(4 * W).bitcast(I32).rearrange("p (k s) -> p k s", s=W)
        masked8 = region[:, at[0] - 4 * W:at[0]].bitcast(U8).rearrange("p (k t s b) -> p k t s b", k=4, s=P, b=4)
        masked16 = region[:, at[0] - 4 * W:at[0]].bitcast(U16).rearrange("p (k s) -> p k s", s=2 * W)
        words16 = region[:, at[0] - 6 * W:at[0] - 4 * W].bitcast(U16).rearrange("p (a s) -> p a s", s=2 * W)
        at[0] = 0
        Abuf = work((RING + 1) * T * P // 4)
        A_s = Abuf.bitcast(F8).rearrange("p (a m s) -> p a m s", m=T, s=P)
        A32_s = Abuf.bitcast(I32).rearrange("p (a w) -> p a w", a=RING + 1)
        AG_s = Abuf.bitcast(BF16).rearrange("p (a m s) -> p a m s", m=T, s=P)
        U = work((RING + 1) * D).rearrange("p (a f) -> p a f", f=D)
        uT = work((RING + 1) * D).rearrange("p (a k n) -> p a k n", k=KC, n=P)
        lo_f = work((RING + 1) * D).rearrange("p (a f) -> p a f", f=D)
        acc_s, hs, Q, Z, Zn, Zg, hf = (work(D) for _ in range(7))
        mean_s = work(D).rearrange("p (k n) -> p k n", k=KC)
        xb = work(RING * D).rearrange("p (a f) -> p a f", f=D)
        bg_s = region[:, RW - LAYERS * D:RW].rearrange("p (l f) -> p l f", f=D)
        assert at[0] == RW and LAYERS * D == (RING + 1) * D
        Wsq = U[:, 0:KC, :]
        iota = sb("iota", [P, P], F16)
        iota_w = sb("iota_w", [P, W], I16)
        ident = sb("ident", [P, P])
        mean_w = sb("mean_w", [P, P])
        ones = sb("ones", [P, P])
        one_b = sb("one_b", [P, 1], BF16)
        zero_b = sb("zero_b", [P, P], BF16)
        tile_base = sb("tile_base", [P, T])
        group_base = sb("group_base", [P, FIELDS])
        valid = sb("valid", [P, T])
        eps_c = sb("eps_c", [P, 1])
        half_c = sb("half_c", [P, 1])
        Win_s = sb("Win_s", [P, KC, D])
        Wl_s = sb("Wl_s", [P, LAYERS * KC, D])
        Wg_s = sb("Wg_s", [P, LAYERS * KC, D])
        bin_s = sb("bin_s", [P, D])
        blg = sb("blg", [P, LAYERS, D])
        gam = sb("gam", [P, LAYERS, D])
        bet = sb("bet", [P, LAYERS, D])
        rowsum = sb("rowsum", [P, 2 * T])
        bad = sb("bad", [P, 3])
        flag = sb("flag", [1, 1], I32)
        degp = sb("degp", [P, T])
        root = sb("root", [P, T])
        dinv = sb("dinv", [P, T])
        gmax = sb("gmax", [P, 2 * LAYERS])
        bound = sb("bound", [P, LAYERS])
        upscale = sb("upscale", [P, LAYERS])
        c_read = sb("c_read", [P, LAYERS * T])
        c_own = sb("c_own", [P, LAYERS * T])
        c_write = sb("c_write", [P, LAYERS * T])
        nmax = sb("nmax", [P, 2])
        nstd = sb("nstd", [P, 1])
        stats_all = sb("stats_all", [P, T, 6])
        mv_all = sb("mv_all", [P, T, 2])
        std_all = sb("std_all", [P, T])
        rstd_all = sb("rstd_all", [P, T])
        st = sb("st", [P, 6])
        mv = sb("mv", [P, 2])
        mv2 = sb("mv2", [P, 2])
        sd = sb("sd", [P, 1])
        rs = sb("rs", [P, 1])
        sd2 = sb("sd2", [P, 1])
        hsum = sb("hsum", [P, D])
        bias = sb("bias", [P, D])
        Wr_s = sb("Wr_s", [P, KC, EX])
        br_s = sb("br_s", [1, EX])
        mcol = sb("mcol", [P, KC])
        ra = sb("ra", [1, 12, EX])
        rscal = sb("rscal", [1, 3, 4])
        topi = sb("topi", [1, EX], U32)
        topw = sb("topw", [P, TOP])
        b1_s = sb("b1_s", [P, TOP, FC])
        b2_s = sb("b2_s", [P, TOP, D])
        b2c = sb("b2c", [P, D])
        fgam = sb("fgam", [P, D])
        fbet = sb("fbet", [P, D])

        bank = [ctx.enter_context(nc.psum_tensor(f"bank{i}", [P, 512], F32)) for i in range(8)]
        T3 = [bank[i][:, 0:D].rearrange("p (k n) -> p k n", k=KC) for i in range(8)]
        acc = [bank[0], bank[1], bank[2], bank[7]]

        raw_set = sem("raw_set")
        edges_in = sem("edges_in")
        wts_in = sem("wts_in")
        x_in = sem("x_in")
        const_set = sem("const_set")
        pool_step = sem("pool_step")
        dve_setup = sem("dve_setup")
        raw_cast = sem("raw_cast")
        edges_T = sem("edges_T")
        before_set = sem("before_set")
        starts_sum = sem("starts_sum")
        hot_ready = sem("hot_ready")
        hot_used = sem("hot_used")
        words_ready = sem("words_ready")
        masks_ready = sem("masks_ready")
        act_staged = sem("act_staged")
        pool_staged = sem("pool_staged")
        a_written = [sem(f"a_written{h}") for h in range(2)]
        deg_done = sem("deg_done")
        bad_set = sem("bad_set")
        bad_sum = sem("bad_sum")
        flag_set = sem("flag_set")
        g_hot = sem("g_hot")
        g_used = sem("g_used")
        g_words = sem("g_words")
        g_masked = sem("g_masked")
        g_staged = sem("g_staged")
        g_written = sem("g_written")
        g_deg = sem("g_deg")
        norms_done = sem("norms_done")
        sqrt_asked = sem("sqrt_asked")
        sqrt_done = sem("sqrt_done")
        wsq_set = sem("wsq_set")
        scales_set = sem("scales_set")
        xn_ready = sem("xn_ready")
        xnT_done = sem("xnT_done")
        xnT_copied = sem("xnT_copied")
        in_mm = sem("in_mm")
        h0_ready = sem("h0_ready")
        hi0_ready = sem("hi0_ready")
        tab_ready = sem("tab_ready")
        hsum_ready = sem("hsum_ready")
        dve_start = sem("dve_start")
        mean_done = sem("mean_done")
        mean_copied = sem("mean_copied")
        ctx_done = sem("ctx_done")
        a_in = [sem(f"a_in{a}") for a in range(RING + 1)]
        plane_in = sem("plane_in")
        plane_used = sem("plane_used")
        agg_done = sem("agg_done")
        lo_ready = sem("lo_ready")
        u_ready = sem("u_ready")
        uT_done = sem("uT_done")
        uT_copied = sem("uT_copied")
        mm_done = sem("mm_done")
        dve_tile = sem("dve_tile")
        var_ready = sem("var_ready")
        std_ready = sem("std_ready")
        h_ready = sem("h_ready")
        hi_ready = sem("hi_ready")
        x2_in = [sem(f"x2_in{u}") for u in range(RING)]
        x1_ready = sem("x1_ready")
        dve_end = sem("dve_end")
        var2_ready = sem("var2_ready")
        std2_ready = sem("std2_ready")
        xsum = sem("xsum")
        xmean_done = sem("xmean_done")
        xmean_copied = sem("xmean_copied")
        logits_done = sem("logits_done")
        dve_route = sem("dve_route")
        exp_asked = sem("exp_asked")
        exp_done = sem("exp_done")
        top_ready = sem("top_ready")
        w_ready = sem("w_ready")
        w_spread = sem("w_spread")
        ew_in = sem("ew_in")
        ew_ready = sem("ew_ready")
        xf_ready = sem("xf_ready")
        xfT_done = sem("xfT_done")
        xfT_copied = sem("xfT_copied")
        up_done = sem("up_done")
        gelu_done = sem("gelu_done")
        down_done = sem("down_done")
        y_taken = sem("y_taken")
        dve_ffn = sem("dve_ffn")
        fvar_ready = sem("fvar_ready")
        pool_ffn = sem("pool_ffn")
        frstd_ready = sem("frstd_ready")
        out_ready = sem("out_ready")
        out_out = [sem(f"out_out{u}") for u in range(RING)]

        block = ctx.enter_context(nc.Block())

        CT = 9
        CE = 4
        CF = 8
        OUT_PER = [16 * (LOOP + 1), 16 * LOOP, 16 * LOOP]

        def spans(f):
            return f * PK, min(PK, T - f * PK)

        def tiles(eng, step, n0):
            step(n0, 0, 0, RING)
            with eng.Fori(0, LOOP) as i:
                for a in range(RING):
                    step(n0 + (i * RING + a + 1), i * RING + a + 1, i, a)

        def tiles3(eng, step):
            with eng.Fori(0, LOOP) as i:
                for u in range(RING):
                    step(i * RING + u, i, u, P)
            step(T - 1, LOOP, 0, LAST)

        def columns(eng, step):
            step(0, 0, 0)
            with eng.Fori(0, MLOOP) as i:
                for k in range(1, 2 * MG + 1):
                    step(i * (2 * MG) + k, k, i)

        def every_word(eng, step):
            with eng.Fori(0, T) as m:
                with eng.Fori(0, FIELDS) as g:
                    step(m * FIELDS + g, m, g)

        def read_flag(eng):
            eng.wait_ge(flag_set, 1)
            return eng.value_load(flag[0:1, 0:1], min_val=0, max_val=1)

        def layers(eng, one):
            with eng.Fori(0, LAYERS - 1) as l:
                one(l, l * T, False)
            one(LAYERS - 1, (LAYERS - 1) * T, True)

        @block.sync
        def _(sp):
            full = (CH - 1) * P * P
            rest = (NE - full) // P
            for h in range(2):
                sp.sem_inc(a_written[h], 16)
            for u in range(RING):
                sp.sem_inc(out_out[u], 16)
            sp.sem_inc(g_written, 16 * PLANES)
            sp.wait_ge(raw_set, 1)
            for raw, v in ((raw_dst, dst), (raw_src, src)):
                sp.dma_start(raw[:, 0:CH - 1, :], v[0:full].rearrange("(k r e) -> r k e", r=P, e=P)).then_inc(edges_in, 16)
                sp.dma_start(raw[0:rest, CH - 1, :],
                             v[full:full + rest * P].rearrange("(r e) -> r e", e=P)).then_inc(edges_in, 16)
                sp.dma_start(raw[rest:rest + 1, CH - 1, 0:NE - full - rest * P],
                             v[full + rest * P:NE].rearrange("(r e) -> r e", r=1)).then_inc(edges_in, 16)
            sp.wait_ge(raw_set, 2)
            sp.dma_start(H[:, 0:T - 1, :], x[0:(T - 1) * P, :].rearrange("(t p) f -> p t f", p=P)).then_inc(x_in, 16)
            sp.dma_start(H[0:LAST, T - 1, :], x[(T - 1) * P:N, :]).then_inc(x_in, 16)
            sp.dma_start(Win_s[:], W_in.rearrange("(k p) f -> p k f", p=P)).then_inc(wts_in, 16)
            sp.dma_start(bin_s[:], b_in.rearrange("(o f) -> o f", o=1).to_broadcast([P, D])).then_inc(wts_in, 16)
            for s, v in ((gam, gamma), (bet, beta), (blg, bl), (bg_s, bg)):
                for l in range(LAYERS):
                    sp.dma_start(s[:, l, :], v[l:l + 1, :].to_broadcast([P, D])).then_inc(wts_in, 16)
            sp.dma_start(Wl_s[:], Wl.rearrange("l (k p) f -> p (l k) f", p=P)).then_inc(wts_in, 16)
            sp.dma_start(Wg_s[:], Wg.rearrange("l (k p) f -> p (l k) f", p=P)).then_inc(wts_in, 16)
            sp.dma_start(Wr_s[:], Wr.rearrange("(k p) e -> p k e", p=P)).then_inc(wts_in, 16)
            sp.dma_start(br_s[:], br.rearrange("(o e) -> o e", o=1)).then_inc(wts_in, 16)
            sp.dma_start(fgam[:], fgamma.rearrange("(o f) -> o f", o=1).to_broadcast([P, D])).then_inc(wts_in, 16)
            sp.dma_start(fbet[:], fbeta.rearrange("(o f) -> o f", o=1).to_broadcast([P, D])).then_inc(wts_in, 16)

            def write(q, h, m0, width):
                sp.wait_ge(act_staged, m0 + width + 1)
                sp.wait_ge(pool_staged, m0 + width + 1)
                sp.dma_start(A[:, :, ds(m0, width), :].rearrange("t p m s -> p t (m s)"),
                             stage32[h][:, :, 0:width, :].rearrange("p t m s -> p t (m s)")).then_inc(a_written[h], 16)
            with sp.Fori(0, MLOOP) as i:
                for h in range(2):
                    write(i * 2 + h, h, i * (2 * MG) + h * MG, MG)
            write(2 * MLOOP, 0, T - 1, 1)
            sp.wait_ge(a_written[0], 16 * (MLOOP + 2))
            sp.wait_ge(a_written[1], 16 * (MLOOP + 1))

            def fast():
                def one(l, n0, last):
                    def load(n, t, i, a):
                        sp.wait_ge(agg_done, n + 1)
                        sp.dma_start(A32_s[:, a, :],
                                     A[ds(t, 1), :, :, :].rearrange("o p m s -> (o p) (m s)")).then_inc(a_in[a], 16)
                    tiles(sp, load, n0)
                with sp.Fori(0, LAYERS) as l:
                    one(l, l * T, False)

            def general():
                def planes(n, m, g):
                    sp.wait_ge(g_staged, n + 2)
                    for k in range(PLANES):
                        sp.dma_start(AG[ds(g * PK, PK), k, :, ds(m, 1), :].rearrange("t p m s -> p t (m s)"),
                                     gstage[:, k, :].rearrange("p (t s) -> p t s", s=P)).then_inc(g_written, 16)
                every_word(sp, planes)
                sp.wait_ge(g_written, 16 * PLANES * (T * FIELDS + 1))
                sp.wait_ge(g_deg, T * FIELDS + 2)
                with sp.Fori(0, LAYERS) as l:
                    with sp.Fori(0, T) as t:
                        with sp.Fori(0, PLANES) as k:
                            hold(sp, plane_used, (l * T + t) * PLANES + k + 1)
                            sp.dma_start(AG_s[:, 0, :, :].rearrange("p m s -> p (m s)"),
                                         AG[ds(t, 1), ds(k, 1), :, :, :].rearrange("o q p m s -> (o q p) (m s)")
                                         ).then_inc(plane_in, 16)
            f = read_flag(sp)
            with sp.If(f == 0):
                fast()
            with sp.Else():
                general()


            sp.wait_ge(top_ready, 1)
            for a in range(TOP):
                e = sp.value_load(topi[0:1, a:a + 1], min_val=0, max_val=EX - 1)
                sp.dma_start(W1_s[:, a * KC:(a + 1) * KC, :],
                             W1[ds(e, 1), :, :].rearrange("o (k p) f -> p (o k) f", p=P)).then_inc(ew_in, 16)
                sp.dma_start(W2_s[:, a, :, :], W2[ds(e, 1), :, :].rearrange("o (p c) f -> p (o c) f", c=FC)).then_inc(ew_in, 16)
                sp.dma_start(b1_s[:, a, :], b1[ds(e, 1), :].rearrange("o (p c) -> (o p) c", c=FC)).then_inc(ew_in, 16)
                sp.dma_start(b2_s[:, a, :], b2[ds(e, 1), :].to_broadcast([P, D])).then_inc(ew_in, 16)

            def store(t, i, u, r):
                sp.wait_ge(out_ready, t + SUP + 1)
                sp.dma_start(out[ds(t * P, r), :], xb[0:r, u, :]).then_inc(out_out[u], 16)
            tiles3(sp, store)
            for u in range(RING):
                sp.wait_ge(out_out[u], OUT_PER[u] + 16)

        @block.gpsimd
        def _(pool):
            own = Steps(pool, pool_step)
            nc.gpsimd.memset(raw_src[:, CH - 1, :], 0)
            own.done(nc.gpsimd.memset(raw_dst[:, CH - 1, :], PADDST))
            own.wait()
            pool.sem_inc(raw_set, 1)
            own.done(nc.gpsimd.memset(H[:, T - 1, :], 0.0))
            own.done(nc.gpsimd.memset(ident[:], 0.0))
            own.done(nc.gpsimd.memset(valid[:], 1.0))
            own.wait()
            pool.sem_inc(raw_set, 1)
            nc.gpsimd.affine_select(out=ident[:], in_=ident[:], compare_op=ALU.not_equal, fill=1.0, base=0,
                                    pattern=[[-1, P]], channel_multiplier=1).then_inc(const_set, 1)
            nc.gpsimd.affine_select(out=valid[:, T - 1:T], in_=valid[:, T - 1:T], compare_op=ALU.is_ge, fill=0.0,
                                    base=LAST - 1, pattern=[[0, 1]], channel_multiplier=-1).then_inc(const_set, 1)
            nc.gpsimd.iota(iota[:], pattern=[[1, P]], base=0, channel_multiplier=0,
                           allow_small_or_imprecise_dtypes=True).then_inc(const_set, 1)
            nc.gpsimd.iota(iota_w[:], pattern=[[1, W]], base=0, channel_multiplier=0,
                           allow_small_or_imprecise_dtypes=True).then_inc(const_set, 1)
            nc.gpsimd.iota(tile_base[:], pattern=[[P, T]], base=0, channel_multiplier=0,
                           allow_small_or_imprecise_dtypes=True).then_inc(const_set, 1)
            nc.gpsimd.iota(group_base[:], pattern=[[W, FIELDS]], base=0, channel_multiplier=0,
                           allow_small_or_imprecise_dtypes=True).then_inc(const_set, 1)
            nc.gpsimd.memset(mean_w[:], 1.0 / N).then_inc(const_set, 1)
            nc.gpsimd.memset(ones[:], 1.0).then_inc(const_set, 1)
            nc.gpsimd.memset(one_b[:], 1.0).then_inc(const_set, 1)
            nc.gpsimd.memset(zero_b[:], 0.0).then_inc(const_set, 1)
            nc.gpsimd.memset(half_c[:], -0.5).then_inc(const_set, 1)

            def unpack(m, k, i):
                h, slot = k // MG % 2, k % MG
                if slot == 0:
                    hold(pool, a_written[h], 16 * (i + k // (2 * MG) + 1))
                    hold(pool, deg_done, m + 1)
                for f in POOL_FIELDS:
                    t0, nt = spans(f)
                    hold(pool, masks_ready, m * 4 + f % 4 + 1)
                    ins = nc.gpsimd.tensor_copy(stage[h][:, t0:t0 + nt, slot, :], masked8[:, f % 4, 0:nt, :, f // 4],
                                                saturate=False)
                ins.then_inc(pool_staged, 1)
            columns(pool, unpack)

            pool.wait_ge(scales_set, 1)
            def again(t, i, u, r):
                hold(pool, x1_ready, t + 1)
                nc.gpsimd.dma_start(xb[0:r, u, :], x[ds(t * P, r), :]).then_inc(x2_in[u], 16)
            tiles3(pool, again)

            def rsqrt(t, i, u, r):
                hold(pool, fvar_ready, t + 1)
                nc.gpsimd.tensor_scalar(sd[0:r, :], mv[0:r, 1:2], EPS, 1.0, ALU.add, ALU.mult).then_inc(pool_ffn, 1)
                hold(pool, pool_ffn, t + 1)
                nc.gpsimd.tensor_tensor(rs[0:r, :], sd[0:r, :], half_c[0:r, :], ALU.pow).then_inc(frstd_ready, 1)
            tiles3(pool, rsqrt)

        @block.vector
        def _(dve):
            v = nc.vector
            own = Steps(dve, dve_setup)

            def magnitude(to, of):
                own.done(v.scalar_tensor_tensor(out=to, in0=of, scalar=-1.0, in1=of, op0=ALU.mult, op1=ALU.max))
            dve.sem_inc(u_ready, RING)
            dve.sem_inc(x1_ready, RING)
            dve.sem_inc(g_masked, 1)
            dve.sem_inc(out_ready, SUP)
            v.memset(eps_c[:], EPS)
            own.done(v.memset(hsum[:], 0.0))
            own.done(v.memset(before[:], 0.0))
            dve.wait_ge(edges_in, 96)
            v.tensor_copy(rawf[:], raw_dst[:]).then_inc(raw_cast, 1)
            dve.wait_ge(raw_cast, 1)
            own.done(v.reduce_max(block_max[:], rawf[:], AX))
            dve.wait_ge(const_set, CONSTS)
            for k in range(CH):
                own.wait()
                own.done(v.scalar_tensor_tensor(out=before[:], in0=tile_base[:], scalar=block_max[:, k:k + 1],
                                                in1=before[:], op0=ALU.is_gt, op1=ALU.add))
            own.wait()
            dve.sem_inc(before_set, 1)
            dve.wait_ge(edges_T, 1)
            own.done(v.tensor_copy(dstf[:, 0:512], bank[0][:, :]))
            own.done(v.tensor_copy(dstf[:, 512:COLS], bank[1][:, 0:COLS - 512]))
            v.tensor_copy(rawf[:], raw_src[:]).then_inc(raw_cast, 1)
            dve.wait_ge(starts_sum, 1)
            own.done(v.tensor_scalar(starts[:], bank[4][0:1, 0:T], float(COLS - WIN), None, ALU.min))
            dve.wait_ge(edges_T, 2)
            own.done(v.tensor_copy(srcf[:, 0:512], bank[2][:, :]))
            own.done(v.tensor_copy(srcf[:, 512:COLS], bank[3][:, 0:COLS - 512]))
            own.done(v.tensor_copy(src_int[:, 0:512], bank[2][:, :]))
            own.done(v.tensor_copy(src_int[:, 512:COLS], bank[3][:, 0:COLS - 512]))
            own.wait()
            own.done(v.tensor_scalar(part_int[:], src_int[:], 7, None, ALU.logical_shift_right))
            own.wait()
            own.done(v.tensor_scalar(field[:], part_int[:], DIV, None, ALU.mult))
            own.wait()
            own.done(v.tensor_scalar(part_int[:], field[:], 10, None, ALU.logical_shift_right))
            own.wait()
            own.done(v.scalar_tensor_tensor(out=src_col[:], in0=part_int[:], scalar=float(-W), in1=srcf[:],
                                            op0=ALU.mult, op1=ALU.add))
            own.done(v.tensor_scalar(field[:], part_int[:], 2, 127, ALU.mult, ALU.add))
            own.wait()
            own.done(v.tensor_scalar(src_w[:].bitcast(I32), field[:], 23, None, ALU.logical_shift_left))
            own.wait()

            def hots(m, k, i):
                start = dve.value_load(starts[0:1, ds(m, 1)], min_val=0, max_val=COLS - WIN)
                for j in range(WIN):
                    dve.wait_ge(hot_used, m * WIN + j + 1)
                    v.tensor_scalar(hot_d[:, j, :], iota[:], tile_base[:, ds(m, 1)], dstf[:, ds(start + j, 1)],
                                    ALU.add, ALU.is_equal)
                    v.tensor_scalar(hot_s[:, j, :], iota_w[:], src_col[:, ds(start + j, 1)],
                                    src_w[:, ds(start + j, 1)], ALU.is_equal, ALU.mult).then_inc(hot_ready, 1)
                    if k and j == 4:
                        mask(m - 1, (k - 1) % 2)

            def mask(m, a):
                dve.wait_ge(words_ready, m + 2)
                dve.wait_ge(act_staged, m + 1)
                dve.wait_ge(pool_staged, m + 1)
                for s in range(4):
                    v.tensor_scalar(masked16[:, s, :], words16[:, a, :], 2 * s, 0x0303, ALU.logical_shift_right,
                                    ALU.bitwise_and).then_inc(masks_ready, 1)
            columns(dve, hots)
            mask(T - 1, (T - 1) % 2)

            dve.wait_ge(deg_done, MG + 1 + T + 1)
            own.done(v.reduce_sum(bad[:, 0:1], bank[6][:, 0:T], AX))
            own.done(v.reduce_max(bad[:, 2:3], rowsum[:], AX))
            own.wait()
            own.done(v.tensor_scalar(bad[:, 1:2], bad[:, 2:3], float(1 << 24), None, ALU.is_ge))
            own.wait()
            dve.sem_inc(bad_set, 1)
            dve.wait_ge(bad_sum, 1)
            own.done(v.tensor_scalar(bad[0:1, 2:3], bank[4][0:1, 0:1], float(NE), None, ALU.not_equal))
            own.wait()
            v.scalar_tensor_tensor(out=flag[:], in0=bank[4][0:1, 1:2], scalar=0.0, in1=bad[0:1, 2:3], op0=ALU.is_gt,
                                   op1=ALU.max).then_inc(flag_set, 1)

            def general():
                def word(n, m, g):
                    with dve.Fori(0, COLS // WIN) as i:
                        for j in range(WIN):
                            q = (n * (COLS // WIN) + i) * WIN + j
                            c = ds(i * WIN + j, 1)
                            dve.wait_ge(g_used, q + 1)
                            v.tensor_scalar(hot_d[:, j, :], iota[:], tile_base[:, ds(m, 1)], dstf[:, c], ALU.add,
                                            ALU.is_equal)
                            v.tensor_scalar(hot_s[:, j, :], iota_w[:], group_base[:, ds(g, 1)], srcf[:, c], ALU.add,
                                            ALU.is_equal).then_inc(g_hot, 1)
                    dve.wait_ge(g_words, n + 2)
                    dve.wait_ge(g_staged, n + 1)
                    for k in range(PLANES):
                        ins = v.tensor_scalar(masked[:, k, :], words[:, 0, :], 0xFF << (8 * k), None, ALU.bitwise_and)
                    ins.then_inc(g_masked, 1)
                every_word(dve, word)
                dve.wait_ge(g_deg, T * FIELDS + 2)
            f = read_flag(dve)
            with dve.If(f == 1):
                general()

            v.tensor_scalar(degp[:], bank[6][:, 0:T], 1.0, None, ALU.add).then_inc(sqrt_asked, 1)
            dve.wait_ge(wts_in, WTS)
            v.tensor_tensor(Wsq, Win_s[:], Win_s[:], ALU.mult).then_inc(wsq_set, 1)
            own.done(v.tensor_tensor(blg[:], blg[:], bg_s[:], ALU.add))
            for k, s in ((0, gam), (LAYERS, bet)):
                own.wait()
                magnitude(lo_f, s[:])
                own.wait()
                own.done(v.reduce_max(gmax[:, k:k + LAYERS], lo_f, AX))
            own.wait()
            own.done(v.scalar_tensor_tensor(out=bound[:, 1:LAYERS], in0=gmax[:, 0:LAYERS - 1], scalar=ROWNORM,
                                            in1=gmax[:, LAYERS:2 * LAYERS - 1], op0=ALU.mult, op1=ALU.add))
            magnitude(lo_f[:, 0, :], bin_s[:])
            own.wait()
            own.done(v.reduce_max(nmax[:, 1:2], lo_f[:, 0, :], AX))
            dve.wait_ge(norms_done, 1)
            v.reduce_max(nmax[:, 0:1], bank[5][:, 0:D], AX).then_inc(sqrt_asked, 1)
            dve.wait_ge(sqrt_done, 2)
            own.done(v.scalar_tensor_tensor(out=bound[:, 0:1], in0=nstd[:], scalar=ROWNORM, in1=nmax[:, 1:2],
                                            op0=ALU.mult, op1=ALU.add))
            own.wait()
            own.done(v.tensor_scalar(bound[:], bound[:], 1e-30, 1.0 / SPAN, ALU.max, ALU.mult))
            own.wait()
            own.done(v.reciprocal(upscale[:], bound[:]))
            own.done(v.reciprocal(dinv[:], root[:]))

            own.wait()
            dve.sem_inc(scales_set, 1)

            dve.wait_ge(x_in, 32)
            with dve.Fori(0, LOOP) as i:
                for u in range(RING):
                    v.bn_stats(stats_all[:, i * RING + u, :], H[:, i * RING + u, :])
            own.done(v.bn_stats(stats_all[:, T - 1, :], H[:, T - 1, :]))
            own.wait()
            me, mo = stats_all[:, :, 1], stats_all[:, :, 4]
            own.done(v.tensor_tensor(mv_all[:, :, 0], me, mo, ALU.add))
            own.done(v.tensor_tensor(std_all[:], me, mo, ALU.subtract))
            own.done(v.tensor_tensor(mv_all[:, :, 1], stats_all[:, :, 2], stats_all[:, :, 5], ALU.add))
            own.wait()
            own.done(v.tensor_scalar(mv_all[:, :, 0], mv_all[:, :, 0], 0.5, None, ALU.mult))
            own.done(v.tensor_tensor(rstd_all[:], std_all[:], std_all[:], ALU.mult))
            own.done(v.tensor_scalar(mv_all[:, :, 1], mv_all[:, :, 1], 1.0 / D, None, ALU.mult))
            own.wait()
            v.scalar_tensor_tensor(out=mv_all[:, :, 1], in0=rstd_all[:], scalar=0.25, in1=mv_all[:, :, 1],
                                   op0=ALU.mult, op1=ALU.add).then_inc(sqrt_asked, 1)
            for l in range(LAYERS):
                own.done(v.tensor_scalar(c_read[:, l * T:(l + 1) * T], dinv[:], bound[:, l:l + 1], None, ALU.mult))
                own.done(v.tensor_scalar(c_own[:, l * T:(l + 1) * T], root[:], bound[:, l:l + 1], None, ALU.mult))
                own.done(v.tensor_scalar(c_write[:, l * T:(l + 1) * T], dinv[:], upscale[:, l:l + 1], None, ALU.mult))
            dve.wait_ge(sqrt_done, 3)
            own.done(v.reciprocal(rstd_all[:], std_all[:]))
            own.wait()

            def xn(t, u):
                v.tensor_scalar(U[:, u, :], H[:, t, :], mv_all[:, t, 0:1], rstd_all[:, ds(t, 1)], ALU.subtract,
                                ALU.mult).then_inc(xn_ready, 1)

            def low(n, to, h, at, made):
                dve.wait_ge(made, n + 1)
                v.scalar_tensor_tensor(out=tab[:, to, D:2 * D], in0=h, scalar=c_write[:, ds(at, 1)],
                                       in1=tab[:, to, 0:D], op0=ALU.mult, op1=ALU.subtract).then_inc(tab_ready, 1)

            def add_rows(t, h):
                return v.scalar_tensor_tensor(out=hsum[:], in0=h, scalar=valid[:, ds(t, 1)], in1=hsum[:],
                                              op0=ALU.mult, op1=ALU.add)

            def in_step(t, u, ahead):
                dve.wait_ge(in_mm, t + 1)
                v.tensor_tensor(lo_f[:, u, :], bank[3 + u][:, 0:D], bin_s[:], ALU.add).then_inc(h0_ready, 1)
                if ahead:
                    xn(t + 2, (u + 2) % RING)
                dve.wait_ge(h0_ready, t + 1)
                add_rows(t, lo_f[:, u, :])
                low(t, t, lo_f[:, u, :], t, hi0_ready)
            xn(0, 0)
            xn(1, 1)
            with dve.Fori(0, LOOP - 1) as i:
                for u in range(RING):
                    in_step(i * RING + u, u, True)
            for t in range(T - 4, T):
                in_step(t, t % RING, t + 2 < T)
            dve.wait_ge(tab_ready, T)
            dve.sem_inc(hsum_ready, 1)

            tile_own = Steps(dve, dve_tile)
            end_own = Steps(dve, dve_end)
            start_own = Steps(dve, dve_start)

            def one(l, n0, last):
                here, there = (l & 1) * T, ((l + 1) & 1) * T
                start_own.at(l * 2)
                dve.wait_ge(ctx_done, l + 1)
                start_own.done(v.tensor_tensor(bias[:], bank[5][:, D:2 * D], blg[:, l, :], ALU.add))
                start_own.done(v.memset(hsum[:], 0.0))
                start_own.hold()

                def step(n, t, i, a):
                    tile_own.at(n * CT)
                    tile_own.done(v.tensor_tensor(hs, tab[:, here + t, 0:D], tab[:, here + t, D:2 * D], ALU.add))
                    dve.wait_ge(lo_ready, n + 1)
                    tile_own.done(v.tensor_tensor(acc_s, acc[a][:, 0:D], lo_f[:, a, :], ALU.add))
                    tile_own.wait()
                    tile_own.done(v.tensor_scalar(Q, acc_s, c_read[:, ds(n, 1)], None, ALU.mult))
                    tile_own.wait()
                    v.scalar_tensor_tensor(out=U[:, 0, :], in0=hs, scalar=c_own[:, ds(n, 1)], in1=Q, op0=ALU.mult,
                                           op1=ALU.add).then_inc(u_ready, 1)
                    dve.wait_ge(mm_done, n + 1)
                    tile_own.done(v.tensor_tensor(Z, bank[4][:, 0:D], bias[:], ALU.add))
                    tile_own.wait()
                    tile_own.done(v.tensor_scalar(Zn, Z, 0.0, None, ALU.max))
                    tile_own.hold()
                    tile_own.done(v.bn_stats(st[:], Zn))
                    tile_own.hold()
                    v.bn_aggr(mv[:], st[:]).then_inc(var_ready, 1)
                    dve.wait_ge(std_ready, n + 1)
                    tile_own.done(v.reciprocal(rs[:], sd[:]))
                    tile_own.wait()
                    tile_own.done(v.tensor_scalar(Z, Zn, mv[:, 0:1], rs[:], ALU.subtract, ALU.mult))
                    tile_own.wait()
                    tile_own.done(v.tensor_tensor(Zg, Z, gam[:, l, :], ALU.mult))
                    tile_own.wait()
                    assert tile_own.k == CT
                    v.tensor_tensor(hf, Zg, bet[:, l, :], ALU.add).then_inc(h_ready, 1)
                    dve.wait_ge(h_ready, n + 1)
                    if not last:
                        add_rows(t, hf)
                        low(n, there + t, hf, n + T, hi_ready)
                        return
                    end_own.at(t * CE)
                    u = (a + 1) % RING if a < RING else 0
                    dve.wait_ge(x2_in[u], 16 * (i + 2) if a == RING - 1 else 16 * (i + 1))
                    v.tensor_tensor(H[:, t, :], hf, xb[:, u, :], ALU.add).then_inc(x1_ready, 1)
                    hold(dve, x1_ready, t + RING + 1)
                    end_own.done(v.bn_stats(st[:], H[:, t, :]))
                    end_own.hold()
                    end_own.done(v.bn_aggr(mv2[:], st[:]))
                    end_own.wait()
                    v.tensor_copy(mv_all[:, t, :], mv2[:]).then_inc(var2_ready, 1)
                    dve.wait_ge(std2_ready, t + 1)
                    end_own.done(v.reciprocal(rstd_all[:, ds(t, 1)], sd2[:]))
                    end_own.wait()
                    end_own.done(v.tensor_scalar(Z, H[:, t, :], mv_all[:, t, 0:1], rstd_all[:, ds(t, 1)],
                                                 ALU.subtract, ALU.mult))
                    end_own.wait()
                    assert end_own.k == CE
                    add_rows(t, Z).then_inc(xsum, 1)
                tiles(dve, step, n0)
                if not last:
                    dve.wait_ge(tab_ready, (l + 2) * T)
                    dve.sem_inc(hsum_ready, 1)
            layers(dve, one)
            dve.wait_ge(xsum, T)
            dve.sem_inc(hsum_ready, 1)

            own = Steps(dve, dve_route)
            dve.wait_ge(logits_done, 1)
            lg, ex, rw, ld, sc, sw, e2, t8 = (ra[:, k, :] for k in range(8))
            own.done(v.tensor_tensor(lg, bank[5][0:1, 0:EX], br_s[:], ALU.add))
            own.wait()

            def softmax(a, b, width, k):
                own.done(v.reduce_max(rscal[:, k, 0:1], a, AX))
                own.wait()
                v.tensor_scalar(rscal[:, k, 1:2], rscal[:, k, 0:1], -1.0, None, ALU.mult).then_inc(exp_asked, 1)
                dve.wait_ge(exp_done, k + 1)
                own.done(v.reciprocal(rscal[:, k, 3:4], rscal[:, k, 2:3]))
                own.wait()
                own.done(v.tensor_scalar(b, ra[:, 8, 0:width], rscal[:, k, 3:4], None, ALU.mult))
                own.wait()
            softmax(lg, rw, EX, 0)
            own.done(v.tensor_scalar(ld, rw, float(N), None, ALU.mult))
            own.wait()
            own.done(v.reciprocal(sc, ld))
            own.wait()
            own.done(v.tensor_scalar(sw, sc, CAPACITY, 1.0, ALU.mult, ALU.min))
            own.wait()
            own.done(v.tensor_tensor(e2, rw, sw, ALU.mult))
            own.wait()
            softmax(e2, ex, EX, 1)
            own.done(v.max(t8, ex))
            own.wait()
            v.max_index(topi[:], t8, ex).then_inc(top_ready, 1)
            softmax(t8[:, 0:TOP], ra[:, 9, 0:TOP], TOP, 2)
            dve.sem_inc(w_ready, 1)
            dve.wait_ge(w_spread, 1)
            own.done(v.tensor_copy(topw[:], bank[5][:, 0:TOP]))
            own.wait()
            dve.wait_ge(ew_in, 16 * 4 * TOP)
            for a in range(TOP):
                own.done(v.tensor_scalar(W2_s[:, a, :, :], W2_s[:, a, :, :], topw[:, a:a + 1], None, ALU.mult))
            own.done(v.tensor_scalar(b2c[:], b2_s[:, 0, :], topw[:, 0:1], None, ALU.mult))
            own.wait()
            own.done(v.scalar_tensor_tensor(out=b2c[:], in0=b2_s[:, 1, :], scalar=topw[:, 1:2], in1=b2c[:],
                                            op0=ALU.mult, op1=ALU.add))
            own.wait()
            dve.sem_inc(ew_ready, 1)

            own = Steps(dve, dve_ffn)

            def xf(t, u, r):
                v.tensor_scalar(U[0:r, u, :], H[0:r, t, :], mv_all[0:r, t, 0:1], rstd_all[0:r, ds(t, 1)], ALU.subtract,
                                ALU.mult).then_inc(xf_ready, 1)

            def result(t, i, u, r):
                own.at(t * CF)
                own.done(v.tensor_scalar(Zn[0:r], H[0:r, t, :], mv_all[0:r, t, 0:1], rstd_all[0:r, ds(t, 1)],
                                         ALU.subtract, ALU.mult))
                dve.wait_ge(down_done, t + 1)
                own.done(v.tensor_tensor(Z[0:r], bank[5 + u][0:r, 0:D], b2c[0:r, :], ALU.add))
                own.wait()
                own.done(v.tensor_tensor(Zg[0:r], Z[0:r], Zn[0:r], ALU.add))
                own.hold()
                own.done(v.bn_stats(st[0:r, :], Zg[0:r]))
                own.hold()
                v.bn_aggr(mv[0:r, :], st[0:r, :]).then_inc(fvar_ready, 1)
                dve.wait_ge(frstd_ready, t + 1)
                own.done(v.tensor_scalar(Z[0:r], Zg[0:r], mv[0:r, 0:1], rs[0:r, :], ALU.subtract, ALU.mult))
                own.wait()
                own.done(v.tensor_tensor(Zn[0:r], Z[0:r], fgam[0:r, :], ALU.mult))
                own.wait()
                own.done(v.tensor_tensor(Zg[0:r], Zn[0:r], fbet[0:r, :], ALU.add))
                own.wait()
                assert own.k == CF - 1
                dve.wait_ge(out_out[u], (i + 1) * 16)
                own.done(v.tensor_tensor(xb[0:r, u, :], Zg[0:r], H[0:r, t, :], ALU.add))
                own.wait()
                dve.sem_inc(out_ready, 1)

            for u in range(SUP):
                xf(u, u, P)
            with dve.Fori(0, LOOP - 1) as i:
                for u in range(SUP):
                    dve.wait_ge(xfT_done, i * SUP + u + 1)
                    xf((i + 1) * SUP + u, u, P)
                for u in range(SUP):
                    result(i * SUP + u, i, u, P)
            dve.wait_ge(xfT_done, T - SUP)
            xf(T - 1, 0, LAST)
            for u in range(SUP):
                result(T - 1 - SUP + u, LOOP - 1, u, P)
            result(T - 1, LOOP, 0, LAST)

        @block.scalar
        def _(act):
            a = nc.scalar

            for s in (act_staged, pool_staged, words_ready, uT_copied, g_words, g_staged):
                act.sem_inc(s, 1)

            def unpack(m, k, i):
                h, slot = k // MG % 2, k % MG
                if slot == 0:
                    act.wait_ge(a_written[h], 16 * (i + k // (2 * MG) + 1))
                    act.wait_ge(deg_done, m + 1)
                for f in ACT_FIELDS:
                    t0, nt = spans(f)
                    hold(act, masks_ready, m * 4 + f % 4 + 1)
                    ins = a.activation(stage[h][:, t0:t0 + nt, slot, :], masked8[:, f % 4, 0:nt, :, f // 4], ACT.Copy,
                                       saturate=False)
                ins.then_inc(act_staged, 1)

            def extract(m, k, i):
                if k:
                    unpack(m - 1, k - 1, i)
                act.wait_ge(hot_used, (m + 2) * WIN)
                for half in range(2):
                    ins = a.activation(words[:, k % 2, half * HALF:(half + 1) * HALF],
                                       bank[k % 2 * 2 + half][:, 0:HALF], ACT.Copy,
                                       accum_out=rowsum[:, ds(m * 2 + half, 1)])
                ins.then_inc(words_ready, 1)
            columns(act, extract)
            unpack(T - 1, 2 * MG, MLOOP - 1)

            def general():
                def word(n, m, g):
                    act.wait_ge(g_used, (n + 1) * COLS + WIN)
                    act.wait_ge(g_masked, n + 1)
                    for half in range(2):
                        ins = a.activation(words[:, 0, half * HALF:(half + 1) * HALF], bank[half][:, 0:HALF], ACT.Copy)
                    ins.then_inc(g_words, 1)
                    act.wait_ge(g_masked, n + 2)
                    act.wait_ge(g_written, (n + 1) * (16 * PLANES))
                    act.wait_ge(g_deg, n + 1)
                    ins = a.activation(gstage, masked[:, 0:PLANES, :], ACT.Copy)
                    ins.then_inc(g_staged, 1)
                every_word(act, word)
            f = read_flag(act)
            with act.If(f == 1):
                general()

            act.wait_ge(sqrt_asked, 1)
            a.activation(root[:], degp[:], ACT.Sqrt).then_inc(sqrt_done, 1)
            act.wait_ge(sqrt_asked, 2)
            a.activation(nstd[:], nmax[:, 0:1], ACT.Sqrt).then_inc(sqrt_done, 1)
            act.wait_ge(sqrt_asked, 3)
            a.activation(std_all[:], mv_all[:, :, 1], ACT.Sqrt, bias=eps_c[:]).then_inc(sqrt_done, 1)

            def high(n, to, h, at, asked, done):
                act.wait_ge(asked, n + 1)
                a.activation(tab[:, to, 0:D], h, ACT.Copy, scale=c_write[:, ds(at, 1)]).then_inc(done, 1)

            def xnT(t, u):
                act.wait_ge(xnT_done, t + 1)
                a.activation(uT[:, u, :, :], T3[u][:, :, :], ACT.Copy).then_inc(xnT_copied, 1)
            xnT(0, 0)
            xnT(1, 1)
            with act.Fori(0, LOOP - 1) as i:
                for u in range(RING):
                    high(i * RING + u, i * RING + u, lo_f[:, u, :], i * RING + u, h0_ready, hi0_ready)
                    xnT(i * RING + u + 2, (u + 2) % RING)
            for t in range(T - 4, T):
                high(t, t, lo_f[:, t % RING, :], t, h0_ready, hi0_ready)
                if t + 2 < T:
                    xnT(t + 2, (t + 2) % RING)

            def one(l, n0, last):
                there = ((l + 1) & 1) * T
                act.wait_ge(mean_done, l + 1)
                a.activation(mean_s, T3[5], ACT.Copy).then_inc(mean_copied, 1)

                def step(n, t, i, s):
                    act.wait_ge(agg_done, n + RING + 1)
                    a.activation(lo_f[:, s, :], acc[s][:, D:2 * D], ACT.Copy).then_inc(lo_ready, 1)
                    act.wait_ge(uT_done, n + 1)
                    a.activation(uT[:, 0, :, :], T3[3], ACT.Copy).then_inc(uT_copied, 1)
                    act.wait_ge(var_ready, n + 1)
                    a.activation(sd[:], mv[:, 1:2], ACT.Sqrt, bias=eps_c[:]).then_inc(std_ready, 1)
                    if not last:
                        high(n, there + t, hf, n + T, h_ready, hi_ready)
                    else:
                        act.wait_ge(var2_ready, t + 1)
                        a.activation(sd2[:], mv_all[:, t, 1:2], ACT.Sqrt, bias=eps_c[:]).then_inc(std2_ready, 1)
                tiles(act, step, n0)
            layers(act, one)

            act.wait_ge(xmean_done, 1)
            a.activation(mcol[:], bank[5][:, 0:KC], ACT.Copy).then_inc(xmean_copied, 1)
            for k, (row, width) in enumerate(((0, EX), (6, EX), (7, TOP))):
                act.wait_ge(exp_asked, k + 1)
                a.activation(ra[:, 8, 0:width], ra[:, row, 0:width], ACT.Exp, bias=rscal[:, k, 1:2],
                             accum_out=rscal[:, k, 2:3]).then_inc(exp_done, 1)

            def xfT_tile(t, u, r):
                act.wait_ge(xfT_done, t + 1)
                a.activation(xfT[:, :, u * P:u * P + r], T3[3 + u % 2][:, :, 0:r], ACT.Copy).then_inc(xfT_copied, 1)

            def gelus(g0, w):
                for f in range(TOP * FC):
                    act.wait_ge(up_done, g0 + f + 1)
                    a.activation(gT[:, f, 0:w], bank[f % 3][:, 0:w], ACT.Gelu,
                                 bias=b1_s[:, f // FC, f % FC:f % FC + 1]).then_inc(gelu_done, 1)
            act.wait_ge(ew_in, 16 * 4 * TOP)
            for u in range(SUP):
                xfT_tile(u, u, P)
            with act.Fori(0, LOOP - 1) as i:
                gelus(i * (TOP * FC), SUP * P)
                for u in range(SUP):
                    xfT_tile((i + 1) * SUP + u, u, P)
            gelus((LOOP - 1) * TOP * FC, SUP * P)
            xfT_tile(T - 1, 0, LAST)
            gelus(LOOP * TOP * FC, LAST)

        @block.tensor
        def _(pe):
            mm = nc.tensor.matmul
            pe.sem_inc(hot_used, WIN)
            pe.sem_inc(g_used, WIN)
            pe.sem_inc(agg_done, RING)
            pe.sem_inc(g_deg, 1)
            pe.sem_inc(plane_used, 1)
            pe.sem_inc(deg_done, MG + 1)

            pe.wait_ge(const_set, CONSTS)
            for s in range(2):
                pe.wait_ge(raw_cast, s + 1)
                for k in range(CH):
                    ins = nc.tensor.transpose(bank[2 * s + k // 4][:, (k % 4) * P:(k % 4 + 1) * P], rawf[:, k, :], ident[:])
                ins.then_inc(edges_T, 1)
                if s == 0:
                    pe.wait_ge(before_set, 1)
                    mm(bank[4][0:1, 0:T], ones[:, 0:1], before[:], start=True, stop=True).then_inc(starts_sum, 1)
            pe.wait_ge(hot_ready, 1)

            def clear(start):
                return mm(bank[6][:, 0:FIELDS * PK], zero_b[:], zero_b[:, 0:FIELDS * PK], start=start, stop=not start)

            def degrees(m, k):
                h, slot = k // MG % 2, k % MG
                pe.wait_ge(act_staged, m + 2)
                hold(pe, pool_staged, m + 2)
                for t in range(T):
                    ins = mm(bank[6][:, t:t + 1], stage[h][:, t, slot, :], one_b[:], start=False, stop=False)
                ins.then_inc(deg_done, 1)

            def counts(m, k, i):
                if k:
                    pe.wait_ge(words_ready, m)
                for j in range(WIN):
                    pe.wait_ge(hot_ready, m * WIN + j + 1)
                    for half in range(2):
                        ins = mm(bank[k % 2 * 2 + half][:, 0:HALF], hot_d[:, j, :],
                                 hot_s[:, j, half * HALF:(half + 1) * HALF], start=j == 0, stop=j == WIN - 1)
                    ins.then_inc(hot_used, 1)
                if k:
                    degrees(m - 1, k - 1)
            clear(True)
            columns(pe, counts)
            degrees(T - 1, 2 * MG)
            clear(False).then_inc(deg_done, 1)
            pe.wait_ge(bad_set, 1)
            mm(bank[4][:, 0:2], ones[:], bad[:, 0:2], start=True, stop=True).then_inc(bad_sum, 1)

            def general():
                def word(n, m, g):
                    pe.wait_ge(g_words, n + 1)

                    def blocks(i, start, stop):
                        for j in range(WIN):
                            q = (n * (COLS // WIN) + i) * WIN + j
                            pe.wait_ge(g_hot, q + 1)
                            for half in range(2):
                                ins = mm(bank[half][:, 0:HALF], hot_d[:, j, :], hot_s[:, j, half * HALF:(half + 1) * HALF],
                                         start=start and j == 0, stop=stop and j == WIN - 1)
                            ins.then_inc(g_used, 1)
                    blocks(0, True, False)
                    with pe.Fori(1, COLS // WIN - 1) as i:
                        blocks(i, False, False)
                    blocks(COLS // WIN - 1, False, True)
                    hold(pe, g_staged, n + 2)
                    for k in range(PLANES):
                        for t in range(PK):
                            ins = mm(bank[6][:, ds(g * PK + t, 1)], gstage[:, k, t * P:(t + 1) * P], one_b[:],
                                     start=False, stop=False)
                    ins.then_inc(g_deg, 1)
                clear(True)
                every_word(pe, word)
                clear(False).then_inc(g_deg, 1)
            f = read_flag(pe)
            with pe.If(f == 1):
                general()

            pe.wait_ge(wsq_set, 1)
            for k in range(KC):
                ins = mm(bank[5][:, 0:D], ones[:], Wsq[:, k, :], start=k == 0, stop=k == KC - 1)
            ins.then_inc(norms_done, 1)

            def turn(t, u):
                pe.wait_ge(xn_ready, t + 1)
                for k in range(KC):
                    ins = nc.tensor.transpose(T3[u][:, k, :], U[:, u, k * P:(k + 1) * P], ident[:])
                ins.then_inc(xnT_done, 1)

            def product(t, u):
                pe.wait_ge(xnT_copied, t + 1)
                for k in range(KC):
                    ins = mm(bank[3 + u][:, 0:D], uT[:, u, k, :], Win_s[:, k, :], start=k == 0, stop=k == KC - 1)
                ins.then_inc(in_mm, 1)
            turn(0, 0)
            turn(1, 1)
            with pe.Fori(0, LOOP - 1) as i:
                for u in range(RING):
                    product(i * RING + u, u)
                    turn(i * RING + u + 2, (u + 2) % RING)
            for t in range(T - 4, T):
                product(t, t % RING)
                if t + 2 < T:
                    turn(t + 2, (t + 2) % RING)

            def turn_u(n):
                pe.wait_ge(u_ready, RING + n + 1)
                pe.wait_ge(uT_copied, n + 1)
                for k in range(KC):
                    ins = nc.tensor.transpose(T3[3][:, k, :], U[:, 0, k * P:(k + 1) * P], ident[:])
                ins.then_inc(uT_done, 1)

            def product_u(n, l):
                pe.wait_ge(uT_copied, n + 2)
                for k in range(KC):
                    ins = mm(bank[4][:, 0:D], uT[:, 0, k, :], Wl_s[:, l * KC + k, :], start=k == 0, stop=k == KC - 1)
                ins.then_inc(mm_done, 1)

            def mean(l):
                pe.wait_ge(hsum_ready, l + 1)
                for k in range(KC):
                    ins = mm(T3[5][:, k, :], hsum[:, k * P:(k + 1) * P], mean_w[:], start=True, stop=True)
                ins.then_inc(mean_done, 1)

            def context(l):
                pe.wait_ge(mean_copied, l + 1)
                for k in range(KC):
                    ins = mm(bank[5][:, D:2 * D], mean_s[:, k, :], Wg_s[:, l * KC + k, :], start=k == 0, stop=k == KC - 1)
                ins.then_inc(ctx_done, 1)

            def fast():
                def aggregate(l, n, a, i, last_l):
                    here = (l & 1) * T
                    if a == RING:
                        pe.wait_ge(tab_ready, (l + 1) * T - 1)
                    pe.wait_ge(u_ready, n + 1)
                    hold(pe, a_in[a], (l + 1) * 16 if a == RING else (l * LOOP + i + 1) * 16)
                    for m in range(T):
                        if last_l is not None and m == BEFORE_T:
                            turn_u(n - 1)
                        if last_l is not None and m == BEFORE_MM:
                            product_u(n - 1, last_l)
                        if a == RING and m == T - 1:
                            mean(l)
                        ins = mm(acc[a][:, :], A_s[:, a, m, :], tab[:, here + m, :], start=m == 0, stop=m == T - 1)
                    ins.then_inc(agg_done, 1)
                    if a == RING:
                        context(l)

                def rest(l):
                    with pe.Fori(0, LOOP) as i:
                        for a in range(RING):
                            aggregate(l, l * T + i * RING + a + 1, a, i, l)
                for l in range(LAYERS):
                    aggregate(l, l * T, RING, 0, l - 1 if l else None)
                    rest(l)
                turn_u(LAYERS * T - 1)
                product_u(LAYERS * T - 1, LAYERS - 1)

            def general():
                def layer(l, here):
                    pe.wait_ge(tab_ready, (l + 1) * T)
                    mean(l)
                    context(l)

                    def step(n, t, i, a):
                        pe.wait_ge(u_ready, n + 1)
                        for k in range(PLANES):
                            pe.wait_ge(plane_in, (n * PLANES + k + 1) * 16)
                            for m in range(T):
                                ins = mm(acc[a][:, :], AG_s[:, 0, m, :], tab[:, here + m, :],
                                         start=k == 0 and m == 0, stop=k == PLANES - 1 and m == T - 1)
                            ins.then_inc(plane_used, 1)
                        pe.wait_ge(plane_used, (n + 1) * PLANES + 1)
                        pe.sem_inc(agg_done, 1)
                        turn_u(n)
                        product_u(n, l)
                    tiles(pe, step, l * T)
                with pe.Fori(0, LAYERS // 2) as q:
                    for k in range(2):
                        layer(q * 2 + k, k * T)
            with pe.If(f == 0):
                fast()
            with pe.Else():
                general()

            pe.wait_ge(hsum_ready, LAYERS + 1)
            for k in range(KC):
                ins = mm(bank[5][:, k:k + 1], hsum[:, k * P:(k + 1) * P], mean_w[:, 0:1], start=True, stop=True)
            ins.then_inc(xmean_done, 1)
            pe.wait_ge(xmean_copied, 1)
            for k in range(KC):
                ins = mm(bank[5][0:1, 0:EX], mcol[:, k:k + 1], Wr_s[:, k, :], start=k == 0, stop=k == KC - 1)
            ins.then_inc(logits_done, 1)
            pe.wait_ge(w_ready, 1)
            mm(bank[5][:, 0:TOP], ones[0:1, :], ra[:, 9, 0:TOP], start=True, stop=True).then_inc(w_spread, 1)

            def turn(t, u, r):
                pe.wait_ge(xf_ready, t + 1)
                if u >= 2:
                    pe.wait_ge(xfT_copied, t - 1)
                for k in range(KC):
                    ins = nc.tensor.transpose(T3[3 + u % 2][:, k, 0:r], U[0:r, u, k * P:(k + 1) * P], ident[0:r, 0:r])
                ins.then_inc(xfT_done, 1)

            def up(s, g0, ntile, w):
                pe.wait_ge(xfT_copied, ntile)
                for f in range(TOP * FC):
                    if f >= 3:
                        pe.wait_ge(gelu_done, g0 + f - 2)
                    for k in range(KC):
                        ins = mm(bank[f % 3][:, 0:w], W1_s[:, f // FC * KC + k, f % FC:FF:FC], xfT[:, k, 0:w],
                                 start=k == 0, stop=k == KC - 1)
                    ins.then_inc(up_done, 1)

            def down(g0, u, r):
                for f in range(TOP * FC):
                    ins = mm(bank[5 + u][0:r, 0:D], gT[:, f, u * P:u * P + r], W2_s[:, f // FC, f % FC, :],
                             start=f == 0, stop=f == TOP * FC - 1)
                ins.then_inc(down_done, 1)
            pe.wait_ge(ew_in, 16 * 4 * TOP)
            pe.wait_ge(ew_ready, 1)
            F8 = TOP * FC
            for u in range(SUP):
                turn(u, u, P)
            with pe.Fori(0, LOOP - 1) as i:
                up(i, i * F8, (i + 1) * SUP, SUP * P)
                for u in range(SUP):
                    turn((i + 1) * SUP + u, u, P)
                pe.wait_ge(gelu_done, (i + 1) * F8)
                for u in range(SUP):
                    pe.wait_ge(out_ready, (i + 1) * SUP)
                    down(i * F8, u, P)
            up(LOOP - 1, (LOOP - 1) * F8, T - 1, SUP * P)
            turn(T - 1, 0, LAST)
            pe.wait_ge(gelu_done, LOOP * F8)
            for u in range(SUP):
                pe.wait_ge(out_ready, T - 1)
                down((LOOP - 1) * F8, u, P)
            up(LOOP, LOOP * F8, T, LAST)
            pe.wait_ge(gelu_done, (LOOP + 1) * F8)
            pe.wait_ge(out_ready, T)
            down(LOOP * F8, 0, LAST)


WTS = 16 * (2 + 4 * LAYERS + 2 + 4)

_INS = ["x", "src", "dst", "L0_gnn_W_in", "L0_gnn_b_in", "L0_gnn_Wl", "L0_gnn_bl", "L0_gnn_Wg", "L0_gnn_bg",
        "L0_gnn_gamma", "L0_gnn_beta", "L0_ffn_Wr", "L0_ffn_br", "L0_ffn_W1", "L0_ffn_b1", "L0_ffn_W2", "L0_ffn_b2",
        "L0_ffn_gamma", "L0_ffn_beta"]


def kernel(**inputs):
    import numpy as np
    import concourse.bacc as bacc
    from concourse.bass_utils import run_bass_kernel_spmd

    nc = bacc.Bacc("TRN2", target_bir_lowering=False, num_devices=1)
    arrays, args = {}, []
    for name in _INS:
        a = np.ascontiguousarray(inputs[name])
        arrays[f"in_{name}"] = a
        args.append(nc.dram_tensor(f"in_{name}", a.shape, mybir.dt.from_np(a.dtype), kind="ExternalInput").ap())
    out = nc.dram_tensor("out", [N, D], F32, kind="ExternalOutput").ap()
    build(nc, *args, out)
    r = run_bass_kernel_spmd(nc, [arrays], core_ids=[0])
    return r.results[0]["out"]
```

```python
import concourse.bass as bass
from concourse import mybir
from contextlib import ExitStack

F32 = mybir.dt.float32
F16 = mybir.dt.float16
BF16 = mybir.dt.bfloat16
F8 = mybir.dt.float8e4
I32 = mybir.dt.int32
I16 = mybir.dt.int16
U32 = mybir.dt.uint32
U16 = mybir.dt.uint16
U8 = mybir.dt.uint8
ALU = mybir.AluOpType
ACT = mybir.ActivationFunctionType
AX = mybir.AxisListType.X
ds = bass.ds

P = 128
N = 6250
NE = 100000
D = 256
KC = D // P
T = -(-N // P)
LAST = N - (T - 1) * P
NB = -(-NE // P)
CH = -(-NB // P)
WIN = 19
COLS = -(-NB // WIN) * WIN
PK = 5
FIELDS = -(-T // PK)
W = PK * P
HALF = W // 2
PARTS = 10
MG = 4
MLOOP = (T - 1) // (2 * MG)
PLANES = 3
RING = 3
LOOP = (T - 1) // RING
LAYERS = 4
SEVEN = 7
assert T % SEVEN == 0
EX, FF, TOP = 8, 512, 2
FC = FF // P
PADDST = (T + 1) * P - P // 2 + 8
EPS = 1e-5
SPAN = 30000.0
ROWNORM = 16.0
CAPACITY = float(-(-N * 5 // (4 * EX)))
DIV = -(-1024 // PK)
CONSTS = 12
SUP = RING
TURN_AT, PRODUCT_AT = 0, 8
BEFORE_T, BEFORE_MM = 14, 24


def hold(eng, sem, value):
    eng.wait_ge(sem, value)
    eng.nop(nofuse=True)


class Steps:

    def __init__(self, eng, sem):
        self.eng, self.sem, self.base, self.k = eng, sem, 0, 0

    def at(self, base):
        self.base, self.k = base, 0

    def done(self, ins):
        ins.then_inc(self.sem, 1)
        self.k += 1

    def wait(self):
        self.eng.wait_ge(self.sem, self.base + self.k)

    def hold(self):
        hold(self.eng, self.sem, self.base + self.k)


def build(nc, x, src, dst, W_in, b_in, Wl, bl, Wg, bg, gamma, beta, Wr, br, W1, b1, W2, b2, fgamma, fbeta, out):
    assert RING * LOOP == T - 1 and 2 * MG * MLOOP == T - 1 and NB <= 2 * 512 and FIELDS <= 10
    A = nc.dram_tensor("adjacency", [T, P, T, P // 4], I32).ap()
    AG = nc.dram_tensor("adjacency_general", [FIELDS * PK, PLANES, P, T, P], BF16).ap()
    ctx = ExitStack()
    with ctx:
        def sb(name, shape, dt=F32):
            return ctx.enter_context(nc.sbuf_tensor(name, shape, dt))

        def sem(name):
            return ctx.enter_context(nc.semaphore(name))

        tab = sb("tab", [P, 2 * T, 2 * D], F16)
        tabf = tab[:, :, :].rearrange("p t f -> p (t f)").bitcast(F32)
        X = tabf[:, 0:T * D].rearrange("p (t f) -> p t f", f=D)
        H = tabf[:, T * D:].rearrange("p (t f) -> p t f", f=D)
        spare = tabf[:, T * D:]
        stage = [spare[:, h * T * P:(h + 1) * T * P].bitcast(F8).rearrange("p (t m s) -> p t m s", m=MG, s=P)
                 for h in range(2)]
        stage32 = [spare[:, h * T * P:(h + 1) * T * P].bitcast(I32).rearrange("p (t m s) -> p t m s", m=MG, s=P // 4)
                   for h in range(2)]
        gstage = spare[:, 0:PLANES * W // 2].bitcast(BF16).rearrange("p (k s) -> p k s", s=W)
        at = [0]

        def part(region, words, size):
            at[0] += words
            assert at[0] <= size
            return region[:, at[0] - words:at[0]]

        def scratch(words, place=None):
            return part(spare if place is None else place, words, T * D)
        raw_src = scratch(CH * P).bitcast(I32).rearrange("p (k e) -> p k e", e=P)
        raw_dst = scratch(CH * P).bitcast(I32).rearrange("p (k e) -> p k e", e=P)
        rawf = scratch(CH * P).rearrange("p (k e) -> p k e", e=P)
        src_int = scratch(COLS).bitcast(I32)
        part_int = scratch(COLS).bitcast(I32)
        field = scratch(COLS).bitcast(I32)
        block_max = scratch(CH)
        before = scratch(T)
        first = tabf[:, 0:T * D]
        at[0] = 0
        W1_s = scratch(TOP * KC * FF, first).rearrange("p (k f) -> p k f", f=FF)
        W2_s = scratch(TOP * FC * D, first).rearrange("p (a c f) -> p a c f", a=TOP, c=FC)
        SUPW = SUP * P
        gT = scratch(TOP * FC * SUPW, first).rearrange("p (f n) -> p f n", f=TOP * FC)
        xfT = scratch(KC * SUPW, first).rearrange("p (k n) -> p k n", k=KC)
        b2_s = scratch(TOP * D, first).rearrange("p (a f) -> p a f", a=TOP)
        b2c = scratch(D, first)
        dstf = sb("dstf", [P, COLS])
        srcf = sb("srcf", [P, COLS])
        src_col = sb("src_col", [P, COLS])
        src_w = sb("src_w", [P, COLS])
        starts = sb("starts", [1, T], I32)
        RW = 11136
        region = sb("region", [P, RW])
        at[0] = 0

        def work(*shape):
            words = 1
            for k in shape:
                words *= k
            return part(region, words, RW)
        hot_s = work(WIN * W // 2).bitcast(BF16).rearrange("p (j s) -> p j s", s=W)
        hot_d = work(WIN * P // 2).bitcast(F16).rearrange("p (s j) -> p s j", j=WIN)
        words = work(2 * W).bitcast(I32).rearrange("p (a s) -> p a s", s=W)
        masked = work(4 * W).bitcast(I32).rearrange("p (k s) -> p k s", s=W)
        masked8 = region[:, at[0] - 4 * W:at[0]].bitcast(U8).rearrange("p (k t s b) -> p k t s b", k=4, s=P, b=4)
        masked16 = region[:, at[0] - 4 * W:at[0]].bitcast(U16).rearrange("p (k s) -> p k s", s=2 * W)
        words16 = region[:, at[0] - 6 * W:at[0] - 4 * W].bitcast(U16).rearrange("p (a s) -> p a s", s=2 * W)
        at[0] = 0
        Abuf = work((RING + 1) * T * P // 4)
        A_s = Abuf.bitcast(F8).rearrange("p (a m s) -> p a m s", m=T, s=P)
        A32_s = Abuf.bitcast(I32).rearrange("p (a w) -> p a w", a=RING + 1)
        AG_s = Abuf.bitcast(BF16).rearrange("p (a m s) -> p a m s", m=T, s=P)
        U = work(RING * D).rearrange("p (a f) -> p a f", f=D)
        uT = work(D).bitcast(F16).rearrange("p (a k n) -> p a k n", k=KC, n=P)
        at[0] += (RING + 1) * D
        Wl_s = region[:, at[0]:at[0] + LAYERS * KC * D].rearrange("p (l k f) -> p l k f", l=LAYERS, k=KC)
        at[0] -= (RING + 1) * D
        lo_f = work((RING + 1) * D).rearrange("p (a f) -> p a f", f=D)
        acc_s, hs, Q, Z, Zn, Zg, hf = (work(D) for _ in range(7))
        mean_s = work(D).rearrange("p (k n) -> p k n", k=KC)
        xb = work(RING * D).rearrange("p (a f) -> p a f", f=D)
        bg_s = region[:, RW - LAYERS * D:RW].rearrange("p (l f) -> p l f", f=D)
        assert at[0] <= RW and LAYERS * D == (RING + 1) * D
        Wsq = U[:, 0:KC, :]
        xnb = sb("xnb", [P, D])
        xnT = sb("xnT", [P, KC, P])
        iota = sb("iota", [P, P], F16)
        rep = sb("rep", [P, P, WIN], F16)
        iota_w = sb("iota_w", [P, W], I16)
        ident = sb("ident", [P, P])
        mean_w = sb("mean_w", [P, P])
        mean_last = sb("mean_last", [P, P])
        ones = sb("ones", [P, P])
        one_b = sb("one_b", [P, 1], BF16)
        zero_b = sb("zero_b", [P, P], BF16)
        tile_base = sb("tile_base", [P, T])
        group_base = sb("group_base", [P, FIELDS])
        valid = sb("valid", [P, T])
        eps_c = sb("eps_c", [P, 1])
        half_c = sb("half_c", [P, 1])
        Win_s = sb("Win_s", [P, KC, D])
        Wx = sb("Wx", [P, 2, LAYERS, KC, D], F16)
        Wg_s = sb("Wg_s", [P, LAYERS * KC, D])
        bin_s = sb("bin_s", [P, D])
        blg = sb("blg", [P, LAYERS, D])
        gam = sb("gam", [P, LAYERS, D])
        bet = sb("bet", [P, LAYERS, D])
        rowsum = sb("rowsum", [P, 2 * T])
        bad = sb("bad", [P, 3])
        flag = sb("flag", [1, 1], I32)
        degp = sb("degp", [P, T])
        root = sb("root", [P, T])
        dinv = sb("dinv", [P, T])
        gmax = sb("gmax", [P, 2 * LAYERS])
        bound = sb("bound", [P, LAYERS])
        upscale = sb("upscale", [P, LAYERS])
        c_read = sb("c_read", [P, T])
        c_own = sb("c_own", [P, T])
        c_back = sb("c_back", [P, LAYERS * T])
        node = sb("node", [P, T])
        wmax = sb("wmax", [P, 2 * LAYERS])
        wbound = sb("wbound", [P, LAYERS])
        wscale = sb("wscale", [P, LAYERS])
        c_write = sb("c_write", [P, LAYERS * T])
        nmax = sb("nmax", [P, 2])
        nstd = sb("nstd", [P, 1])
        mv_all = sb("mv_all", [P, T, 2])
        rstd_all = sb("rstd_all", [P, T])
        st = sb("st", [P, 6])
        mv = sb("mv", [P, 2])
        mv2 = sb("mv2", [P, 2])
        drel = sb("drel", [P, WIN], F16)
        xst = sb("xst", [P, 6])
        xmv = sb("xmv", [P, 2])
        xsd = sb("xsd", [P, 1])
        xrs = sb("xrs", [P, 1])
        xnb_bias = sb("xnb_bias", [P, 1])
        sd = sb("sd", [P, 1])
        rs = sb("rs", [P, 1])
        sd2 = sb("sd2", [P, 1])
        hsum = sb("hsum", [P, D])
        bias = sb("bias", [P, D])
        Wr_s = sb("Wr_s", [P, KC, EX])
        br_s = sb("br_s", [1, EX])
        mcol = sb("mcol", [P, KC])
        ra = sb("ra", [1, 12, EX])
        rscal = sb("rscal", [1, 3, 4])
        topi = sb("topi", [1, EX], U32)
        topw = sb("topw", [P, TOP])
        b1_s = sb("b1_s", [P, TOP, FC])
        fgam = sb("fgam", [P, D])
        fbet = sb("fbet", [P, D])

        bank = [ctx.enter_context(nc.psum_tensor(f"bank{i}", [P, 512], F32)) for i in range(8)]
        T3 = [bank[i][:, 0:D].rearrange("p (k n) -> p k n", k=KC) for i in range(8)]
        acc = [bank[0], bank[1], bank[2], bank[7]]

        raw_set = sem("raw_set")
        edges_in = sem("edges_in")
        wts_in = sem("wts_in")
        x0_in = sem("x0_in")
        x_in = sem("x_in")
        const_set = sem("const_set")
        pool_step = sem("pool_step")
        dve_setup = sem("dve_setup")
        raw_cast = sem("raw_cast")
        edges_T = sem("edges_T")
        before_set = sem("before_set")
        starts_sum = sem("starts_sum")
        hot_ready = sem("hot_ready")
        hot_used = sem("hot_used")
        words_ready = sem("words_ready")
        masks_ready = sem("masks_ready")
        staged = sem("staged")
        a_written = [sem(f"a_written{h}") for h in range(2)]
        deg_done = sem("deg_done")
        bad_set = sem("bad_set")
        bad_sum = sem("bad_sum")
        flag_set = sem("flag_set")
        g_hot = sem("g_hot")
        g_used = sem("g_used")
        g_words = sem("g_words")
        g_masked = sem("g_masked")
        g_staged = sem("g_staged")
        g_written = sem("g_written")
        g_deg = sem("g_deg")
        norms_done = sem("norms_done")
        sqrt_asked = sem("sqrt_asked")
        sqrt_done = sem("sqrt_done")
        wsq_set = sem("wsq_set")
        scales_set = sem("scales_set")
        dve_x = sem("dve_x")
        xvar_ready = sem("xvar_ready")
        xstd_ready = sem("xstd_ready")
        xscale_ready = sem("xscale_ready")
        xn_ready = sem("xn_ready")
        xnT_done = sem("xnT_done")
        xnT_copied = sem("xnT_copied")
        in_mm = sem("in_mm")
        h0_ready = sem("h0_ready")
        h0_summed = sem("h0_summed")
        hi0_ready = sem("hi0_ready")
        tab_ready = sem("tab_ready")
        hsum_ready = sem("hsum_ready")
        dve_start = sem("dve_start")
        mean_done = sem("mean_done")
        mean_copied = sem("mean_copied")
        ctx_done = sem("ctx_done")
        a_in = [sem(f"a_in{a}") for a in range(RING + 1)]
        plane_in = sem("plane_in")
        plane_used = sem("plane_used")
        agg_done = sem("agg_done")
        lo_ready = sem("lo_ready")
        u_ready = sem("u_ready")
        uT_done = sem("uT_done")
        uT_copied = sem("uT_copied")
        uT_split = sem("uT_split")
        wl_in = sem("wl_in")
        wmax_set = sem("wmax_set")
        wsum_done = sem("wsum_done")
        wscale_set = sem("wscale_set")
        whi_done = sem("whi_done")
        wx_ready = sem("wx_ready")
        mm_done = sem("mm_done")
        dve_tile = sem("dve_tile")
        var_ready = sem("var_ready")
        std_ready = sem("std_ready")
        h_ready = sem("h_ready")
        hi_ready = sem("hi_ready")
        x2_in = [sem(f"x2_in{u}") for u in range(RING)]
        x1_ready = sem("x1_ready")
        dve_end = sem("dve_end")
        var2_ready = sem("var2_ready")
        std2_ready = sem("std2_ready")
        xsum = sem("xsum")
        xmean_done = sem("xmean_done")
        xmean_copied = sem("xmean_copied")
        logits_done = sem("logits_done")
        dve_route = sem("dve_route")
        exp_asked = sem("exp_asked")
        exp_done = sem("exp_done")
        top_ready = sem("top_ready")
        w_ready = sem("w_ready")
        w_spread = sem("w_spread")
        w1_in = sem("w1_in")
        w2_in = sem("w2_in")
        ew_ready = sem("ew_ready")
        xf_ready = sem("xf_ready")
        xfT_done = sem("xfT_done")
        xfT_copied = sem("xfT_copied")
        up_done = sem("up_done")
        gelu_done = sem("gelu_done")
        down_done = sem("down_done")
        y_taken = sem("y_taken")
        dve_ffn = sem("dve_ffn")
        fvar_ready = sem("fvar_ready")
        pool_ffn = sem("pool_ffn")
        frstd_ready = sem("frstd_ready")
        out_ready = sem("out_ready")
        out_out = [sem(f"out_out{u}") for u in range(RING)]

        block = ctx.enter_context(nc.Block())

        CX = 3
        CT = 9
        CE = 4
        CF = 8
        OUT_PER = [16 * (LOOP + 1), 16 * LOOP, 16 * LOOP]

        def spans(f):
            return f * PK, min(PK, T - f * PK)

        def tiles(eng, step, n0):
            step(n0, 0, 0, RING)
            with eng.Fori(0, LOOP) as i:
                for a in range(RING):
                    step(n0 + (i * RING + a + 1), i * RING + a + 1, i, a)

        def tiles3(eng, step):
            with eng.Fori(0, LOOP) as i:
                for u in range(RING):
                    step(i * RING + u, i, u, P)
            step(T - 1, LOOP, 0, LAST)

        def columns(eng, step):
            step(0, 0, 0)
            with eng.Fori(0, MLOOP) as i:
                for k in range(1, 2 * MG + 1):
                    step(i * (2 * MG) + k, k, i)

        def every_word(eng, step):
            with eng.Fori(0, T) as m:
                with eng.Fori(0, FIELDS) as g:
                    step(m * FIELDS + g, m, g)

        def read_flag(eng):
            eng.wait_ge(flag_set, 1)
            return eng.value_load(flag[0:1, 0:1], min_val=0, max_val=1)

        def layers(eng, one):
            with eng.Fori(0, LAYERS - 1) as l:
                one(l, l * T, False)
            one(LAYERS - 1, (LAYERS - 1) * T, True)

        @block.sync
        def _(sp):
            full = (CH - 1) * P * P
            rest = (NE - full) // P
            for h in range(2):
                sp.sem_inc(a_written[h], 16)
            for u in range(RING):
                sp.sem_inc(out_out[u], 16)
            sp.sem_inc(g_written, 16 * PLANES)
            sp.wait_ge(raw_set, 1)
            for raw, v in ((raw_dst, dst), (raw_src, src)):
                sp.dma_start(raw[:, 0:CH - 1, :], v[0:full].rearrange("(k r e) -> r k e", r=P, e=P)).then_inc(edges_in, 16)
                sp.dma_start(raw[0:rest, CH - 1, :],
                             v[full:full + rest * P].rearrange("(r e) -> r e", e=P)).then_inc(edges_in, 16)
                sp.dma_start(raw[rest:rest + 1, CH - 1, 0:NE - full - rest * P],
                             v[full + rest * P:NE].rearrange("(r e) -> r e", r=1)).then_inc(edges_in, 16)
            sp.dma_start(Win_s[:], W_in.rearrange("(k p) f -> p k f", p=P)).then_inc(wts_in, 16)
            sp.dma_start(bin_s[:], b_in.rearrange("(o f) -> o f", o=1).to_broadcast([P, D])).then_inc(wts_in, 16)
            for s, v in ((gam, gamma), (bet, beta), (blg, bl), (bg_s, bg)):
                for l in range(LAYERS):
                    sp.dma_start(s[:, l, :], v[l:l + 1, :].to_broadcast([P, D])).then_inc(wts_in, 16)
            sp.dma_start(Wg_s[:], Wg.rearrange("l (k p) f -> p (l k) f", p=P)).then_inc(wts_in, 16)
            sp.dma_start(Wr_s[:], Wr.rearrange("(k p) e -> p k e", p=P)).then_inc(wts_in, 16)
            sp.dma_start(br_s[:], br.rearrange("(o e) -> o e", o=1)).then_inc(wts_in, 16)
            sp.dma_start(fgam[:], fgamma.rearrange("(o f) -> o f", o=1).to_broadcast([P, D])).then_inc(wts_in, 16)
            sp.dma_start(fbet[:], fbeta.rearrange("(o f) -> o f", o=1).to_broadcast([P, D])).then_inc(wts_in, 16)

            sp.wait_ge(raw_set, 2)
            sp.dma_start(X[:, 0, :], x[0:P, :]).then_inc(x0_in, 16)
            sp.dma_start(X[:, 1:T - 1, :], x[P:(T - 1) * P, :].rearrange("(t p) f -> p t f", p=P)).then_inc(x_in, 16)
            sp.dma_start(X[0:LAST, T - 1, :], x[(T - 1) * P:N, :]).then_inc(x_in, 16)

            def write(h, m0, width):
                sp.wait_ge(staged, m0 + width + 1)
                sp.dma_start(A[:, :, ds(m0, width), :].rearrange("t p m s -> p t (m s)"),
                             stage32[h][:, :, 0:width, :].rearrange("p t m s -> p t (m s)")).then_inc(a_written[h], 16)
            with sp.Fori(0, MLOOP) as i:
                for h in range(2):
                    write(h, i * (2 * MG) + h * MG, MG)
            write(0, T - 1, 1)
            sp.wait_ge(a_written[0], 16 * (MLOOP + 2))
            sp.wait_ge(a_written[1], 16 * (MLOOP + 1))

            def layer_weights():
                sp.dma_start(Wl_s, Wl.rearrange("l (k p) f -> p l k f", p=P)).then_inc(wl_in, 16)

            def fast():
                layer_weights()

                def one(l, n0, last):
                    def load(n, t, i, a):
                        sp.wait_ge(agg_done, n + 1)
                        sp.dma_start(A32_s[:, a, :],
                                     A[ds(t, 1), :, :, :].rearrange("o p m s -> (o p) (m s)")).then_inc(a_in[a], 16)
                    tiles(sp, load, n0)
                with sp.Fori(0, LAYERS) as l:
                    one(l, l * T, False)

            def general():
                def planes(n, m, g):
                    sp.wait_ge(g_staged, n + 2)
                    for k in range(PLANES):
                        sp.dma_start(AG[ds(g * PK, PK), k, :, ds(m, 1), :].rearrange("t p m s -> p t (m s)"),
                                     gstage[:, k, :].rearrange("p (t s) -> p t s", s=P)).then_inc(g_written, 16)
                every_word(sp, planes)
                sp.wait_ge(g_written, 16 * PLANES * (T * FIELDS + 1))
                sp.wait_ge(g_deg, T * FIELDS + 2)
                layer_weights()
                with sp.Fori(0, LAYERS) as l:
                    with sp.Fori(0, T) as t:
                        with sp.Fori(0, PLANES) as k:
                            hold(sp, plane_used, (l * T + t) * PLANES + k + 1)
                            sp.dma_start(AG_s[:, 0, :, :].rearrange("p m s -> p (m s)"),
                                         AG[ds(t, 1), ds(k, 1), :, :, :].rearrange("o q p m s -> (o q p) (m s)")
                                         ).then_inc(plane_in, 16)
            f = read_flag(sp)
            with sp.If(f == 0):
                fast()
            with sp.Else():
                general()


            sp.wait_ge(top_ready, 1)
            chosen = [sp.value_load(topi[0:1, a:a + 1], min_val=0, max_val=EX - 1) for a in range(TOP)]
            for a, e in enumerate(chosen):
                sp.dma_start(W1_s[:, a * KC:(a + 1) * KC, :],
                             W1[ds(e, 1), :, :].rearrange("o (k p) f -> p (o k) f", p=P)).then_inc(w1_in, 16)
                sp.dma_start(b1_s[:, a, :], b1[ds(e, 1), :].rearrange("o (p c) -> (o p) c", c=FC)).then_inc(w1_in, 16)
            for a, e in enumerate(chosen):
                sp.dma_start(W2_s[:, a, :, :], W2[ds(e, 1), :, :].rearrange("o (p c) f -> p (o c) f", c=FC)).then_inc(w2_in, 16)
                sp.dma_start(b2_s[:, a, :], b2[ds(e, 1), :].to_broadcast([P, D])).then_inc(w2_in, 16)

            def store(t, i, u, r):
                sp.wait_ge(out_ready, t + SUP + 1)
                sp.dma_start(out[ds(t * P, r), :], xb[0:r, u, :]).then_inc(out_out[u], 16)
            tiles3(sp, store)
            for u in range(RING):
                sp.wait_ge(out_out[u], OUT_PER[u] + 16)

        @block.gpsimd
        def _(pool):
            own = Steps(pool, pool_step)
            nc.gpsimd.memset(raw_src[:, CH - 1, :], 0)
            own.done(nc.gpsimd.memset(raw_dst[:, CH - 1, :], PADDST))
            own.wait()
            pool.sem_inc(raw_set, 1)
            own.done(nc.gpsimd.memset(X[:, T - 1, :], 0.0))
            own.done(nc.gpsimd.memset(ident[:], 0.0))
            own.done(nc.gpsimd.memset(valid[:], 1.0))
            own.wait()
            pool.sem_inc(raw_set, 1)
            nc.gpsimd.affine_select(out=ident[:], in_=ident[:], compare_op=ALU.not_equal, fill=1.0, base=0,
                                    pattern=[[-1, P]], channel_multiplier=1).then_inc(const_set, 1)
            nc.gpsimd.affine_select(out=valid[:, T - 1:T], in_=valid[:, T - 1:T], compare_op=ALU.is_ge, fill=0.0,
                                    base=LAST - 1, pattern=[[0, 1]], channel_multiplier=-1).then_inc(const_set, 1)
            nc.gpsimd.iota(iota[:], pattern=[[1, P]], base=0, channel_multiplier=0,
                           allow_small_or_imprecise_dtypes=True).then_inc(const_set, 1)
            nc.gpsimd.iota(iota_w[:], pattern=[[1, W]], base=0, channel_multiplier=0,
                           allow_small_or_imprecise_dtypes=True).then_inc(const_set, 1)
            nc.gpsimd.iota(tile_base[:], pattern=[[P, T]], base=0, channel_multiplier=0,
                           allow_small_or_imprecise_dtypes=True).then_inc(const_set, 1)
            nc.gpsimd.iota(group_base[:], pattern=[[W, FIELDS]], base=0, channel_multiplier=0,
                           allow_small_or_imprecise_dtypes=True).then_inc(const_set, 1)
            nc.gpsimd.memset(mean_w[:], 1.0 / N).then_inc(const_set, 1)
            nc.gpsimd.memset(ones[:], 1.0).then_inc(const_set, 1)
            nc.gpsimd.memset(one_b[:], 1.0).then_inc(const_set, 1)
            nc.gpsimd.memset(zero_b[:], 0.0).then_inc(const_set, 1)
            nc.gpsimd.memset(half_c[:], -0.5).then_inc(const_set, 1)
            nc.gpsimd.iota(rep[:], pattern=[[1, P], [0, WIN]], base=0, channel_multiplier=0,
                           allow_small_or_imprecise_dtypes=True).then_inc(const_set, 1)

            pool.wait_ge(tab_ready, T)
            def again(t, i, u, r):
                hold(pool, x1_ready, t + 1)
                nc.gpsimd.dma_start(xb[0:r, u, :], x[ds(t * P, r), :]).then_inc(x2_in[u], 16)
            tiles3(pool, again)

            def rsqrt(t, i, u, r):
                hold(pool, fvar_ready, t + 1)
                nc.gpsimd.tensor_scalar(sd[0:r, :], mv[0:r, 1:2], EPS, 1.0, ALU.add, ALU.mult).then_inc(pool_ffn, 1)
                hold(pool, pool_ffn, t + 1)
                nc.gpsimd.tensor_tensor(rs[0:r, :], sd[0:r, :], half_c[0:r, :], ALU.pow).then_inc(frstd_ready, 1)
            tiles3(pool, rsqrt)

        @block.vector
        def _(dve):
            v = nc.vector
            own = Steps(dve, dve_setup)

            def magnitude(to, of):
                own.done(v.scalar_tensor_tensor(out=to, in0=of, scalar=-1.0, in1=of, op0=ALU.mult, op1=ALU.max))
            dve.sem_inc(u_ready, RING)
            dve.sem_inc(x1_ready, RING)
            dve.sem_inc(g_masked, 1)
            dve.sem_inc(out_ready, SUP)
            v.memset(eps_c[:], EPS)
            own.done(v.memset(hsum[:], 0.0))
            own.done(v.memset(before[:], 0.0))
            dve.wait_ge(edges_in, 96)
            v.tensor_copy(rawf[:], raw_dst[:]).then_inc(raw_cast, 1)
            dve.wait_ge(raw_cast, 1)
            own.done(v.reduce_max(block_max[:], rawf[:], AX))
            dve.wait_ge(const_set, CONSTS)
            for k in range(CH):
                own.wait()
                own.done(v.scalar_tensor_tensor(out=before[:], in0=tile_base[:], scalar=block_max[:, k:k + 1],
                                                in1=before[:], op0=ALU.is_gt, op1=ALU.add))
            own.wait()
            dve.sem_inc(before_set, 1)
            dve.wait_ge(edges_T, 1)
            own.done(v.tensor_copy(dstf[:, 0:512], bank[0][:, :]))
            own.done(v.tensor_copy(dstf[:, 512:COLS], bank[1][:, 0:COLS - 512]))
            v.tensor_copy(rawf[:], raw_src[:]).then_inc(raw_cast, 1)
            dve.wait_ge(starts_sum, 1)
            own.done(v.tensor_scalar(starts[:], bank[4][0:1, 0:T], float(COLS - WIN), None, ALU.min))
            dve.wait_ge(edges_T, 2)
            own.done(v.tensor_copy(srcf[:, 0:512], bank[2][:, :]))
            own.done(v.tensor_copy(srcf[:, 512:COLS], bank[3][:, 0:COLS - 512]))
            own.done(v.tensor_copy(src_int[:, 0:512], bank[2][:, :]))
            own.done(v.tensor_copy(src_int[:, 512:COLS], bank[3][:, 0:COLS - 512]))
            own.wait()
            own.done(v.tensor_scalar(part_int[:], src_int[:], 7, None, ALU.logical_shift_right))
            own.wait()
            own.done(v.tensor_scalar(field[:], part_int[:], DIV, None, ALU.mult))
            own.wait()
            own.done(v.tensor_scalar(part_int[:], field[:], 10, None, ALU.logical_shift_right))
            own.wait()
            own.done(v.scalar_tensor_tensor(out=src_col[:], in0=part_int[:], scalar=float(-W), in1=srcf[:],
                                            op0=ALU.mult, op1=ALU.add))
            own.done(v.tensor_scalar(field[:], part_int[:], 2, 127, ALU.mult, ALU.add))
            own.wait()
            own.done(v.tensor_scalar(src_w[:].bitcast(I32), field[:], 23, None, ALU.logical_shift_left))
            own.wait()

            dve.wait_ge(wts_in, WTS)
            own.done(v.tensor_tensor(blg[:], blg[:], bg_s[:], ALU.add))
            own.done(v.tensor_scalar(mean_last[:], mean_w[:], valid[:, T - 1:T], None, ALU.mult))
            own.wait()

            x_own = Steps(dve, dve_x)

            def hots(m, k, i):
                start = dve.value_load(starts[0:1, ds(m, 1)], min_val=0, max_val=COLS - WIN)
                x_own.at(m * CX)
                x_own.done(v.tensor_scalar(drel[:], dstf[:, ds(start, WIN)], tile_base[:, ds(m, 1)], None, ALU.subtract))

                def hot_part(j0, j1):
                    if k or j0:
                        dve.wait_ge(hot_used, m * WIN + j1)
                    return v.tensor_tensor(hot_d[:, :, j0:j1], rep[:, :, j0:j1],
                                           drel[:, j0:j1].unsqueeze(1).to_broadcast([P, P, j1 - j0]), ALU.is_equal)
                for j in range(WIN):
                    if j == PARTS:
                        hot_part(PARTS, WIN)
                    dve.wait_ge(hot_used, m * WIN + j + 1)
                    ins = v.tensor_scalar(hot_s[:, j, :], iota_w[:], src_col[:, ds(start + j, 1)],
                                          src_w[:, ds(start + j, 1)], ALU.is_equal, ALU.mult)
                    if j == 0:
                        x_own.wait()
                        ins = hot_part(0, PARTS)
                    ins.then_inc(hot_ready, 1)
                    if j == 1:
                        dve.wait_ge(x_in if k else x0_in, 32 if k else 16)
                        x_own.done(v.bn_stats(xst[:], X[:, m, :]))
                    if j == 2:
                        x_own.hold()
                        v.bn_aggr(xmv[:], xst[:]).then_inc(xvar_ready, 1)
                    if k and j == 4:
                        mask(m - 1, (k - 1) % 2)
                    if j == 10:
                        dve.wait_ge(xstd_ready, m + 1)
                        if k:
                            dve.wait_ge(xn_ready, m)
                        x_own.done(v.reciprocal(xrs[:], xsd[:]))
                    if j == 11:
                        x_own.wait()
                        v.tensor_scalar(xnb_bias[:], xmv[:, 0:1], xrs[:], -1.0, ALU.mult, ALU.mult).then_inc(xscale_ready, 1)
                assert x_own.k == CX

            def mask(m, a):
                dve.wait_ge(words_ready, m + 2)
                dve.wait_ge(staged, m + 1)
                for s in range(4):
                    v.tensor_scalar(masked16[:, s, :], words16[:, a, :], 2 * s, 0x0303, ALU.logical_shift_right,
                                    ALU.bitwise_and).then_inc(masks_ready, 1)
            columns(dve, hots)
            mask(T - 1, (T - 1) % 2)
            dve.wait_ge(masks_ready, 4 * T)

            v.tensor_tensor(Wsq, Win_s[:], Win_s[:], ALU.mult).then_inc(wsq_set, 1)
            for k, s in ((0, gam), (LAYERS, bet)):
                own.wait()
                magnitude(lo_f, s[:])
                own.wait()
                own.done(v.reduce_max(gmax[:, k:k + LAYERS], lo_f, AX))
            own.wait()
            own.done(v.scalar_tensor_tensor(out=bound[:, 1:LAYERS], in0=gmax[:, 0:LAYERS - 1], scalar=ROWNORM,
                                            in1=gmax[:, LAYERS:2 * LAYERS - 1], op0=ALU.mult, op1=ALU.add))
            magnitude(lo_f[:, 0, :], bin_s[:])
            own.wait()
            own.done(v.reduce_max(nmax[:, 1:2], lo_f[:, 0, :], AX))
            dve.wait_ge(norms_done, 1)
            v.reduce_max(nmax[:, 0:1], bank[2][:, 0:D], AX).then_inc(sqrt_asked, 1)

            dve.wait_ge(deg_done, MG + 1 + T + 1)
            own.done(v.reduce_sum(bad[:, 0:1], bank[6][:, 0:T], AX))
            own.done(v.reduce_max(bad[:, 2:3], rowsum[:], AX))
            own.wait()
            own.done(v.tensor_scalar(bad[:, 1:2], bad[:, 2:3], float(1 << 24), None, ALU.is_ge))
            own.wait()
            dve.sem_inc(bad_set, 1)
            dve.wait_ge(bad_sum, 1)
            own.done(v.tensor_scalar(bad[0:1, 2:3], bank[4][0:1, 0:1], float(NE), None, ALU.not_equal))
            own.wait()
            v.scalar_tensor_tensor(out=flag[:], in0=bank[4][0:1, 1:2], scalar=0.0, in1=bad[0:1, 2:3], op0=ALU.is_gt,
                                   op1=ALU.max).then_inc(flag_set, 1)

            def general():
                def word(n, m, g):
                    with dve.Fori(0, COLS // WIN) as i:
                        for j in range(WIN):
                            q = (n * (COLS // WIN) + i) * WIN + j
                            c = ds(i * WIN + j, 1)
                            dve.wait_ge(g_used, q + 1)
                            v.tensor_scalar(hot_d[:, :, j], iota[:], tile_base[:, ds(m, 1)], dstf[:, c], ALU.add,
                                            ALU.is_equal)
                            v.tensor_scalar(hot_s[:, j, :], iota_w[:], group_base[:, ds(g, 1)], srcf[:, c], ALU.add,
                                            ALU.is_equal).then_inc(g_hot, 1)
                    dve.wait_ge(g_words, n + 2)
                    dve.wait_ge(g_staged, n + 1)
                    for k in range(PLANES):
                        ins = v.tensor_scalar(masked[:, k, :], words[:, 0, :], 0xFF << (8 * k), None, ALU.bitwise_and)
                    ins.then_inc(g_masked, 1)
                every_word(dve, word)
                dve.wait_ge(g_deg, T * FIELDS + 2)
            f = read_flag(dve)
            with dve.If(f == 1):
                general()

            v.tensor_scalar(degp[:], bank[6][:, 0:T], 1.0, None, ALU.add).then_inc(sqrt_asked, 1)
            dve.wait_ge(sqrt_done, 1)
            own.done(v.scalar_tensor_tensor(out=bound[:, 0:1], in0=nstd[:], scalar=ROWNORM, in1=nmax[:, 1:2],
                                            op0=ALU.mult, op1=ALU.add))
            own.wait()
            own.done(v.tensor_scalar(bound[:], bound[:], 1e-30, 1.0 / SPAN, ALU.max, ALU.mult))
            own.wait()
            own.done(v.reciprocal(upscale[:], bound[:]))
            own.wait()
            dve.wait_ge(sqrt_done, 2)
            own.done(v.reciprocal(dinv[:], root[:]))
            own.wait()
            own.done(v.tensor_scalar(c_write[:, 0:T], dinv[:], upscale[:, 0:1], None, ALU.mult))
            own.wait()
            dve.sem_inc(scales_set, 1)
            for l in range(1, LAYERS):
                own.done(v.tensor_scalar(c_write[:, l * T:(l + 1) * T], dinv[:], upscale[:, l:l + 1], None, ALU.mult))
            own.done(v.tensor_scalar(node[:], root[:], 1.0, None, ALU.add))
            own.wait()
            own.done(v.reciprocal(c_back[:, 0:T], node[:]))
            own.wait()
            own.done(v.tensor_tensor(c_read[:], dinv[:], c_back[:, 0:T], ALU.mult))
            own.done(v.tensor_tensor(c_own[:], root[:], c_back[:, 0:T], ALU.mult))
            own.wait()

            def low(n, to, h, at, made):
                dve.wait_ge(made, n + 1)
                v.scalar_tensor_tensor(out=tab[:, to, D:2 * D], in0=h, scalar=c_write[:, ds(at, 1)],
                                       in1=tab[:, to, 0:D], op0=ALU.mult, op1=ALU.subtract).then_inc(tab_ready, 1)

            def add_rows(t, h):
                return v.scalar_tensor_tensor(out=hsum[:], in0=h, scalar=valid[:, ds(t, 1)], in1=hsum[:],
                                              op0=ALU.mult, op1=ALU.add)

            def first_low(t):
                low(t, T + t, X[:, t, :], t, hi0_ready)
            with dve.Fori(0, T // SEVEN) as i:
                for k in range(SEVEN):
                    first_low(i * SEVEN + k)
            dve.wait_ge(h0_summed, 1)
            own.done(v.tensor_copy(hsum[:], bank[5][:, D:2 * D]))
            own.wait()
            dve.wait_ge(tab_ready, T)
            dve.sem_inc(hsum_ready, 1)

            dve.wait_ge(wl_in, 16)
            for l in range(LAYERS):
                own.done(v.reduce_max(wmax[:, l:l + 1], Wl_s[:, l, :, :].rearrange("p k f -> p (k f)"), AX))
                own.done(v.tensor_reduce(wmax[:, LAYERS + l:LAYERS + l + 1],
                                         Wl_s[:, l, :, :].rearrange("p k f -> p (k f)"), AX, ALU.min))
            own.wait()
            v.scalar_tensor_tensor(out=wbound[:], in0=wmax[:, LAYERS:], scalar=-1.0, in1=wmax[:, 0:LAYERS],
                                   op0=ALU.mult, op1=ALU.max).then_inc(wmax_set, 1)
            dve.wait_ge(wsum_done, 1)
            own.done(v.tensor_scalar(wbound[:], bank[6][:, 0:LAYERS], 1e-30, 1.0 / SPAN, ALU.max, ALU.mult))
            own.wait()
            v.reciprocal(wscale[:], wbound[:]).then_inc(wscale_set, 1)
            own.done(v.tensor_tensor(wmax[:, 0:LAYERS], wbound[:], bound[:], ALU.mult))
            own.wait()
            for l in range(LAYERS):
                own.done(v.tensor_scalar(c_back[:, l * T:(l + 1) * T], node[:], wmax[:, l:l + 1], None, ALU.mult))
            for l in range(LAYERS):
                dve.wait_ge(whi_done, l + 1)
                own.done(v.scalar_tensor_tensor(out=Wx[:, 1, l, :, :], in0=Wl_s[:, l, :, :], scalar=wscale[:, l:l + 1],
                                                in1=Wx[:, 0, l, :, :], op0=ALU.mult, op1=ALU.subtract))
            own.wait()
            dve.sem_inc(wx_ready, 1)

            tile_own = Steps(dve, dve_tile)
            end_own = Steps(dve, dve_end)
            start_own = Steps(dve, dve_start)

            def one(l, n0, last):
                here, there = ((l + 1) & 1) * T, (l & 1) * T
                start_own.at(l * 2)
                dve.wait_ge(ctx_done, l + 1)
                start_own.done(v.tensor_tensor(bias[:], bank[5][:, D:2 * D], blg[:, l, :], ALU.add))
                start_own.done(v.memset(hsum[:], 0.0))
                start_own.hold()

                def step(n, t, i, a):
                    tile_own.at(n * CT)
                    tile_own.done(v.tensor_tensor(hs, tab[:, here + t, 0:D], tab[:, here + t, D:2 * D], ALU.add))
                    dve.wait_ge(lo_ready, n + 1)
                    tile_own.done(v.tensor_tensor(acc_s, acc[a][:, 0:D], lo_f[:, a, :], ALU.add))
                    tile_own.wait()
                    tile_own.done(v.tensor_scalar(Q, acc_s, c_read[:, ds(t, 1)], None, ALU.mult))
                    tile_own.wait()
                    v.scalar_tensor_tensor(out=U[:, 0, :], in0=hs, scalar=c_own[:, ds(t, 1)], in1=Q, op0=ALU.mult,
                                           op1=ALU.add).then_inc(u_ready, 1)
                    dve.wait_ge(uT_copied, n + 2)
                    v.tensor_tensor(uT[:, 1, :, :], T3[3], uT[:, 0, :, :], ALU.subtract).then_inc(uT_split, 1)
                    dve.wait_ge(mm_done, n + 1)
                    tile_own.done(v.scalar_tensor_tensor(out=Z, in0=bank[4][:, 0:D], scalar=c_back[:, ds(n, 1)],
                                                         in1=bias[:], op0=ALU.mult, op1=ALU.add))
                    tile_own.wait()
                    tile_own.done(v.tensor_scalar(Zn, Z, 0.0, None, ALU.max))
                    tile_own.hold()
                    tile_own.done(v.bn_stats(st[:], Zn))
                    tile_own.hold()
                    v.bn_aggr(mv[:], st[:]).then_inc(var_ready, 1)
                    dve.wait_ge(std_ready, n + 1)
                    tile_own.done(v.reciprocal(rs[:], sd[:]))
                    tile_own.wait()
                    tile_own.done(v.tensor_scalar(Z, Zn, mv[:, 0:1], rs[:], ALU.subtract, ALU.mult))
                    tile_own.wait()
                    tile_own.done(v.tensor_tensor(Zg, Z, gam[:, l, :], ALU.mult))
                    tile_own.wait()
                    assert tile_own.k == CT
                    v.tensor_tensor(hf, Zg, bet[:, l, :], ALU.add).then_inc(h_ready, 1)
                    dve.wait_ge(h_ready, n + 1)
                    if not last:
                        add_rows(t, hf)
                        low(n, there + t, hf, n + T, hi_ready)
                        return
                    end_own.at(t * CE)
                    u = (a + 1) % RING if a < RING else 0
                    dve.wait_ge(x2_in[u], 16 * (i + 2) if a == RING - 1 else 16 * (i + 1))
                    v.tensor_tensor(H[:, t, :], hf, xb[:, u, :], ALU.add).then_inc(x1_ready, 1)
                    hold(dve, x1_ready, t + RING + 1)
                    end_own.done(v.bn_stats(st[:], H[:, t, :]))
                    end_own.hold()
                    end_own.done(v.bn_aggr(mv2[:], st[:]))
                    end_own.wait()
                    v.tensor_copy(mv_all[:, t, :], mv2[:]).then_inc(var2_ready, 1)
                    dve.wait_ge(std2_ready, t + 1)
                    end_own.done(v.reciprocal(rstd_all[:, ds(t, 1)], sd2[:]))
                    end_own.wait()
                    end_own.done(v.tensor_scalar(Z, H[:, t, :], mv_all[:, t, 0:1], rstd_all[:, ds(t, 1)],
                                                 ALU.subtract, ALU.mult))
                    end_own.wait()
                    assert end_own.k == CE
                    add_rows(t, Z).then_inc(xsum, 1)
                tiles(dve, step, n0)
                if not last:
                    dve.wait_ge(tab_ready, (l + 2) * T)
                    dve.sem_inc(hsum_ready, 1)
            layers(dve, one)
            dve.wait_ge(xsum, T)
            dve.sem_inc(hsum_ready, 1)

            own = Steps(dve, dve_route)
            dve.wait_ge(logits_done, 1)
            lg, ex, rw, ld, sc, sw, e2, t8 = (ra[:, k, :] for k in range(8))
            own.done(v.tensor_tensor(lg, bank[5][0:1, 0:EX], br_s[:], ALU.add))
            own.wait()

            def softmax(a, b, width, k):
                own.done(v.reduce_max(rscal[:, k, 0:1], a, AX))
                own.wait()
                v.tensor_scalar(rscal[:, k, 1:2], rscal[:, k, 0:1], -1.0, None, ALU.mult).then_inc(exp_asked, 1)
                dve.wait_ge(exp_done, k + 1)
                own.done(v.reciprocal(rscal[:, k, 3:4], rscal[:, k, 2:3]))
                own.wait()
                own.done(v.tensor_scalar(b, ra[:, 8, 0:width], rscal[:, k, 3:4], None, ALU.mult))
                own.wait()
            softmax(lg, rw, EX, 0)
            own.done(v.tensor_scalar(ld, rw, float(N), None, ALU.mult))
            own.wait()
            own.done(v.reciprocal(sc, ld))
            own.wait()
            own.done(v.tensor_scalar(sw, sc, CAPACITY, 1.0, ALU.mult, ALU.min))
            own.wait()
            own.done(v.tensor_tensor(e2, rw, sw, ALU.mult))
            own.wait()
            softmax(e2, ex, EX, 1)
            own.done(v.max(t8, ex))
            own.wait()
            v.max_index(topi[:], t8, ex).then_inc(top_ready, 1)
            softmax(t8[:, 0:TOP], ra[:, 9, 0:TOP], TOP, 2)
            dve.sem_inc(w_ready, 1)
            dve.wait_ge(w_spread, 1)
            own.done(v.tensor_copy(topw[:], bank[5][:, 0:TOP]))
            own.wait()
            route_own, own = own, Steps(dve, dve_ffn)

            def xf(t, u, r):
                v.tensor_scalar(U[0:r, u, :], H[0:r, t, :], mv_all[0:r, t, 0:1], rstd_all[0:r, ds(t, 1)], ALU.subtract,
                                ALU.mult).then_inc(xf_ready, 1)

            def result(t, i, u, r):
                own.at(t * CF)
                own.done(v.tensor_scalar(Zn[0:r], H[0:r, t, :], mv_all[0:r, t, 0:1], rstd_all[0:r, ds(t, 1)],
                                         ALU.subtract, ALU.mult))
                dve.wait_ge(down_done, t + 1)
                own.done(v.tensor_tensor(Z[0:r], bank[5 + u][0:r, 0:D], b2c[0:r, :], ALU.add))
                own.wait()
                own.done(v.tensor_tensor(Zg[0:r], Z[0:r], Zn[0:r], ALU.add))
                own.hold()
                own.done(v.bn_stats(st[0:r, :], Zg[0:r]))
                own.hold()
                v.bn_aggr(mv[0:r, :], st[0:r, :]).then_inc(fvar_ready, 1)
                dve.wait_ge(frstd_ready, t + 1)
                own.done(v.tensor_scalar(Z[0:r], Zg[0:r], mv[0:r, 0:1], rs[0:r, :], ALU.subtract, ALU.mult))
                own.wait()
                own.done(v.tensor_tensor(Zn[0:r], Z[0:r], fgam[0:r, :], ALU.mult))
                own.wait()
                own.done(v.tensor_tensor(Zg[0:r], Zn[0:r], fbet[0:r, :], ALU.add))
                own.wait()
                assert own.k == CF - 1
                dve.wait_ge(out_out[u], (i + 1) * 16)
                own.done(v.tensor_tensor(xb[0:r, u, :], Zg[0:r], H[0:r, t, :], ALU.add))
                own.wait()
                dve.sem_inc(out_ready, 1)

            for u in range(SUP):
                xf(u, u, P)
            dve.wait_ge(w2_in, 16 * 2 * TOP)
            for a in range(TOP):
                route_own.done(v.tensor_scalar(W2_s[:, a, :, :], W2_s[:, a, :, :], topw[:, a:a + 1], None, ALU.mult))
            route_own.done(v.tensor_scalar(b2c[:], b2_s[:, 0, :], topw[:, 0:1], None, ALU.mult))
            route_own.wait()
            route_own.done(v.scalar_tensor_tensor(out=b2c[:], in0=b2_s[:, 1, :], scalar=topw[:, 1:2], in1=b2c[:],
                                            op0=ALU.mult, op1=ALU.add))
            route_own.wait()
            dve.sem_inc(ew_ready, 1)
            with dve.Fori(0, LOOP - 1) as i:
                for u in range(SUP):
                    dve.wait_ge(xfT_done, i * SUP + u + 1)
                    xf((i + 1) * SUP + u, u, P)
                for u in range(SUP):
                    result(i * SUP + u, i, u, P)
            dve.wait_ge(xfT_done, T - SUP)
            xf(T - 1, 0, LAST)
            for u in range(SUP):
                result(T - 1 - SUP + u, LOOP - 1, u, P)
            result(T - 1, LOOP, 0, LAST)

        @block.scalar
        def _(act):
            a = nc.scalar

            for s in (staged, words_ready, uT_copied, uT_split, g_words, g_staged):
                act.sem_inc(s, 1)

            def unpack(m, k, i):
                h, slot = k // MG % 2, k % MG
                if slot == 0:
                    act.wait_ge(a_written[h], 16 * (i + k // (2 * MG) + 1))
                    act.wait_ge(deg_done, m + 1)
                for f in sorted(range(FIELDS), key=lambda f: f % 4):
                    t0, nt = spans(f)
                    if f < 4:
                        hold(act, masks_ready, m * 4 + f + 1)
                    ins = a.activation(stage[h][:, t0:t0 + nt, slot, :], masked8[:, f % 4, 0:nt, :, f // 4], ACT.Copy,
                                       saturate=False)
                ins.then_inc(staged, 1)

            def h0(t):
                hold(act, in_mm, t + 1)
                a.activation(X[:, t, :], bank[7][:, 0:D], ACT.Copy).then_inc(h0_ready, 1)

            def extract(m, k, i):
                act.wait_ge(xvar_ready, m + 1)
                a.activation(xsd[:], xmv[:, 1:2], ACT.Sqrt, bias=eps_c[:]).then_inc(xstd_ready, 1)
                if k:
                    act.wait_ge(xnT_done, m)
                    a.activation(xnT[:], T3[4], ACT.Copy).then_inc(xnT_copied, 1)
                    unpack(m - 1, k - 1, i)
                hold(act, xscale_ready, m + 1)
                a.activation(xnb[:], X[:, m, :], ACT.Identity, scale=xrs[:], bias=xnb_bias[:]).then_inc(xn_ready, 1)
                if k:
                    h0(m - 1)
                act.wait_ge(hot_used, (m + 2) * WIN)
                for half in range(2):
                    ins = a.activation(words[:, k % 2, half * HALF:(half + 1) * HALF],
                                       bank[k % 2 * 2 + half][:, 0:HALF], ACT.Copy,
                                       accum_out=rowsum[:, ds(m * 2 + half, 1)])
                ins.then_inc(words_ready, 1)
            columns(act, extract)
            unpack(T - 1, 2 * MG, MLOOP - 1)
            act.wait_ge(xnT_done, T)
            a.activation(xnT[:], T3[4], ACT.Copy).then_inc(xnT_copied, 1)
            h0(T - 1)
            act.wait_ge(sqrt_asked, 1)
            a.activation(nstd[:], nmax[:, 0:1], ACT.Sqrt).then_inc(sqrt_done, 1)

            def general():
                act.wait_ge(a_written[0], 16 * (MLOOP + 2))
                act.wait_ge(a_written[1], 16 * (MLOOP + 1))

                def word(n, m, g):
                    act.wait_ge(g_used, (n + 1) * COLS + WIN)
                    act.wait_ge(g_masked, n + 1)
                    for half in range(2):
                        ins = a.activation(words[:, 0, half * HALF:(half + 1) * HALF], bank[half][:, 0:HALF], ACT.Copy)
                    ins.then_inc(g_words, 1)
                    act.wait_ge(g_masked, n + 2)
                    act.wait_ge(g_written, (n + 1) * (16 * PLANES))
                    act.wait_ge(g_deg, n + 1)
                    ins = a.activation(gstage, masked[:, 0:PLANES, :], ACT.Copy)
                    ins.then_inc(g_staged, 1)
                every_word(act, word)
                act.wait_ge(g_written, 16 * PLANES * (T * FIELDS + 1))
            f = read_flag(act)
            with act.If(f == 1):
                general()

            act.wait_ge(sqrt_asked, 2)
            a.activation(root[:], degp[:], ACT.Sqrt).then_inc(sqrt_done, 1)

            def high(n, to, h, at, asked, done):
                act.wait_ge(asked, n + 1)
                a.activation(tab[:, to, 0:D], h, ACT.Copy, scale=c_write[:, ds(at, 1)]).then_inc(done, 1)

            act.wait_ge(a_written[0], 16 * (MLOOP + 2))
            act.wait_ge(a_written[1], 16 * (MLOOP + 1))
            act.wait_ge(scales_set, 1)
            with act.Fori(0, T // SEVEN) as i:
                for k in range(SEVEN):
                    t = i * SEVEN + k
                    a.activation(tab[:, T + t, 0:D], X[:, t, :], ACT.Copy, scale=c_write[:, ds(t, 1)]).then_inc(hi0_ready, 1)

            act.wait_ge(wscale_set, 1)
            for l in range(LAYERS):
                a.activation(Wx[:, 0, l, :, :], Wl_s[:, l, :, :], ACT.Copy, scale=wscale[:, l:l + 1]).then_inc(whi_done, 1)
            act.wait_ge(wx_ready, 1)

            def one(l, n0, last):
                there = (l & 1) * T
                act.wait_ge(mean_done, l + 1)
                a.activation(mean_s, T3[5], ACT.Copy).then_inc(mean_copied, 1)

                def step(n, t, i, s):
                    act.wait_ge(agg_done, n + RING + 1)
                    a.activation(lo_f[:, s, :], acc[s][:, D:2 * D], ACT.Copy).then_inc(lo_ready, 1)
                    act.wait_ge(uT_done, n + 1)
                    a.activation(uT[:, 0, :, :], T3[3], ACT.Copy).then_inc(uT_copied, 1)
                    act.wait_ge(var_ready, n + 1)
                    a.activation(sd[:], mv[:, 1:2], ACT.Sqrt, bias=eps_c[:]).then_inc(std_ready, 1)
                    if not last:
                        high(n, there + t, hf, n + T, h_ready, hi_ready)
                    else:
                        act.wait_ge(var2_ready, t + 1)
                        a.activation(sd2[:], mv_all[:, t, 1:2], ACT.Sqrt, bias=eps_c[:]).then_inc(std2_ready, 1)
                tiles(act, step, n0)
            layers(act, one)

            act.wait_ge(xmean_done, 1)
            a.activation(mcol[:], bank[5][:, 0:KC], ACT.Copy).then_inc(xmean_copied, 1)
            for k, (row, width) in enumerate(((0, EX), (6, EX), (7, TOP))):
                act.wait_ge(exp_asked, k + 1)
                a.activation(ra[:, 8, 0:width], ra[:, row, 0:width], ACT.Exp, bias=rscal[:, k, 1:2],
                             accum_out=rscal[:, k, 2:3]).then_inc(exp_done, 1)

            def xfT_tile(t, u, r):
                act.wait_ge(xfT_done, t + 1)
                a.activation(xfT[:, :, u * P:u * P + r], T3[3 + u % 2][:, :, 0:r], ACT.Copy).then_inc(xfT_copied, 1)

            def gelus(g0, w):
                for f in range(TOP * FC):
                    act.wait_ge(up_done, g0 + f + 1)
                    a.activation(gT[:, f, 0:w], bank[f % 3][:, 0:w], ACT.Gelu,
                                 bias=b1_s[:, f // FC, f % FC:f % FC + 1]).then_inc(gelu_done, 1)
            for u in range(SUP):
                xfT_tile(u, u, P)
            act.wait_ge(w1_in, 16 * 2 * TOP)
            with act.Fori(0, LOOP - 1) as i:
                gelus(i * (TOP * FC), SUP * P)
                for u in range(SUP):
                    xfT_tile((i + 1) * SUP + u, u, P)
            gelus((LOOP - 1) * TOP * FC, SUP * P)
            xfT_tile(T - 1, 0, LAST)
            gelus(LOOP * TOP * FC, LAST)

        @block.tensor
        def _(pe):
            mm = nc.tensor.matmul
            pe.sem_inc(hot_used, WIN)
            pe.sem_inc(g_used, WIN)
            pe.sem_inc(agg_done, RING)
            pe.sem_inc(g_deg, 1)
            pe.sem_inc(plane_used, 1)
            pe.sem_inc(deg_done, MG + 1)

            pe.wait_ge(const_set, CONSTS)
            for s in range(2):
                pe.wait_ge(raw_cast, s + 1)
                for k in range(CH):
                    ins = nc.tensor.transpose(bank[2 * s + k // 4][:, (k % 4) * P:(k % 4 + 1) * P], rawf[:, k, :], ident[:])
                ins.then_inc(edges_T, 1)
                if s == 0:
                    pe.wait_ge(before_set, 1)
                    mm(bank[4][0:1, 0:T], ones[:, 0:1], before[:], start=True, stop=True).then_inc(starts_sum, 1)
            pe.wait_ge(hot_ready, 1)

            def clear(start):
                return mm(bank[6][:, 0:FIELDS * PK], zero_b[:], zero_b[:, 0:FIELDS * PK], start=start, stop=not start)

            def degrees(m, k):
                h, slot = k // MG % 2, k % MG
                hold(pe, staged, m + 2)
                for t in range(T):
                    ins = mm(bank[6][:, t:t + 1], stage[h][:, t, slot, :], one_b[:], start=False, stop=False)
                ins.then_inc(deg_done, 1)

            def counts(m, k, i):
                if k:
                    pe.wait_ge(words_ready, m)
                for j in range(WIN):
                    if k and j == TURN_AT:
                        turn(m - 1)
                    if k and j == PRODUCT_AT:
                        product(m - 1)
                    pe.wait_ge(hot_ready, m * WIN + j + 1)
                    for half in range(2):
                        ins = mm(bank[k % 2 * 2 + half][:, 0:HALF], hot_d[:, :, j],
                                 hot_s[:, j, half * HALF:(half + 1) * HALF], start=j == 0, stop=j == WIN - 1)
                    ins.then_inc(hot_used, 1)
                if k:
                    degrees(m - 1, k - 1)
                    add_mean(m - 1, mean_w)

            def turn(t):
                pe.wait_ge(xn_ready, t + 1)
                for k in range(KC):
                    ins = nc.tensor.transpose(T3[4][:, k, :], xnb[:, k * P:(k + 1) * P], ident[:])
                ins.then_inc(xnT_done, 1)

            def product(t):
                pe.wait_ge(xnT_copied, t + 1)
                mm(bank[7][:, 0:D], ones[0:1, :], bin_s[0:1, :], start=True, stop=False)
                for k in range(KC):
                    ins = mm(bank[7][:, 0:D], xnT[:, k, :], Win_s[:, k, :], start=False, stop=k == KC - 1)
                ins.then_inc(in_mm, 1)

            def add_mean(t, weights):
                pe.wait_ge(h0_ready, t + 1)
                return mm(bank[5][:, D:2 * D], weights[:], X[:, t, :], start=False,
                          stop=isinstance(t, int) and t == T - 1)
            for k in range(KC):
                mm(bank[5][:, D + k * P:D + (k + 1) * P], zero_b[:], zero_b[:], start=k == 0, stop=False)
            clear(True)
            columns(pe, counts)
            turn(T - 1)
            pe.wait_ge(wsq_set, 1)
            for k in range(KC):
                ins = mm(bank[2][:, 0:D], ones[:], Wsq[:, k, :], start=k == 0, stop=k == KC - 1)
            ins.then_inc(norms_done, 1)
            degrees(T - 1, 2 * MG)
            product(T - 1)
            add_mean(T - 1, mean_last).then_inc(h0_summed, 1)
            clear(False).then_inc(deg_done, 1)
            pe.wait_ge(bad_set, 1)
            mm(bank[4][:, 0:2], ones[:], bad[:, 0:2], start=True, stop=True).then_inc(bad_sum, 1)

            def general():
                def word(n, m, g):
                    pe.wait_ge(g_words, n + 1)

                    def blocks(i, start, stop):
                        for j in range(WIN):
                            q = (n * (COLS // WIN) + i) * WIN + j
                            pe.wait_ge(g_hot, q + 1)
                            for half in range(2):
                                ins = mm(bank[half][:, 0:HALF], hot_d[:, :, j], hot_s[:, j, half * HALF:(half + 1) * HALF],
                                         start=start and j == 0, stop=stop and j == WIN - 1)
                            ins.then_inc(g_used, 1)
                    blocks(0, True, False)
                    with pe.Fori(1, COLS // WIN - 1) as i:
                        blocks(i, False, False)
                    blocks(COLS // WIN - 1, False, True)
                    hold(pe, g_staged, n + 2)
                    for k in range(PLANES):
                        for t in range(PK):
                            ins = mm(bank[6][:, ds(g * PK + t, 1)], gstage[:, k, t * P:(t + 1) * P], one_b[:],
                                     start=False, stop=False)
                    ins.then_inc(g_deg, 1)
                clear(True)
                every_word(pe, word)
                clear(False).then_inc(g_deg, 1)
            f = read_flag(pe)
            with pe.If(f == 1):
                general()

            def turn_u(n):
                pe.wait_ge(u_ready, RING + n + 1)
                pe.wait_ge(uT_split, n + 1)
                for k in range(KC):
                    ins = nc.tensor.transpose(T3[3][:, k, :], U[:, 0, k * P:(k + 1) * P], ident[:])
                ins.then_inc(uT_done, 1)

            def product_u(n, l):
                if l == 0:
                    pe.wait_ge(wx_ready, 1)
                pe.wait_ge(uT_split, n + 2)
                parts = [(a, b, k) for a, b in ((0, 0), (0, 1), (1, 0)) for k in range(KC)]
                for q, (a, b, k) in enumerate(parts):
                    ins = mm(bank[4][:, 0:D], uT[:, a, k, :], Wx[:, b, l, k, :], start=q == 0, stop=q == len(parts) - 1)
                ins.then_inc(mm_done, 1)

            def mean(l):
                pe.wait_ge(hsum_ready, l + 1)
                for k in range(KC):
                    ins = mm(T3[5][:, k, :], hsum[:, k * P:(k + 1) * P], mean_w[:] if l else ident[:], start=True,
                             stop=True)
                ins.then_inc(mean_done, 1)
                if l == 0:
                    pe.wait_ge(wmax_set, 1)
                    mm(bank[6][:, 0:LAYERS], ones[:], wbound[:], start=True, stop=True).then_inc(wsum_done, 1)

            def context(l):
                pe.wait_ge(mean_copied, l + 1)
                for k in range(KC):
                    ins = mm(bank[5][:, D:2 * D], mean_s[:, k, :], Wg_s[:, l * KC + k, :], start=k == 0, stop=k == KC - 1)
                ins.then_inc(ctx_done, 1)

            def fast():
                def aggregate(l, n, a, i, last_l):
                    here = ((l + 1) & 1) * T
                    if a == RING and l:
                        pe.wait_ge(tab_ready, (l + 1) * T - 1)
                    pe.wait_ge(u_ready, n + 1)
                    hold(pe, a_in[a], (l + 1) * 16 if a == RING else (l * LOOP + i + 1) * 16)
                    for m in range(T):
                        if last_l is not None and m == BEFORE_T:
                            turn_u(n - 1)
                        if last_l is not None and m == BEFORE_MM:
                            product_u(n - 1, last_l)
                        if a == RING and l == 0:
                            pe.wait_ge(tab_ready, m + 1)
                        if a == RING and m == T - 1:
                            mean(l)
                        ins = mm(acc[a][:, :], A_s[:, a, m, :], tab[:, here + m, :], start=m == 0, stop=m == T - 1)
                    ins.then_inc(agg_done, 1)
                    if a == RING:
                        context(l)

                def rest(l):
                    with pe.Fori(0, LOOP) as i:
                        for a in range(RING):
                            aggregate(l, l * T + i * RING + a + 1, a, i, l)
                for l in range(LAYERS):
                    aggregate(l, l * T, RING, 0, l - 1 if l else None)
                    rest(l)
                turn_u(LAYERS * T - 1)
                product_u(LAYERS * T - 1, LAYERS - 1)

            def general():
                def layer(l, here):
                    pe.wait_ge(tab_ready, (l + 1) * T)
                    mean(l)
                    context(l)

                    def step(n, t, i, a):
                        pe.wait_ge(u_ready, n + 1)
                        for k in range(PLANES):
                            pe.wait_ge(plane_in, (n * PLANES + k + 1) * 16)
                            for m in range(T):
                                ins = mm(acc[a][:, :], AG_s[:, 0, m, :], tab[:, here + m, :],
                                         start=k == 0 and m == 0, stop=k == PLANES - 1 and m == T - 1)
                            ins.then_inc(plane_used, 1)
                        pe.wait_ge(plane_used, (n + 1) * PLANES + 1)
                        pe.sem_inc(agg_done, 1)
                        turn_u(n)
                        product_u(n, l)
                    tiles(pe, step, l * T)
                for l in range(LAYERS):
                    layer(l, (l + 1) % 2 * T)
            with pe.If(f == 0):
                fast()
            with pe.Else():
                general()

            pe.wait_ge(hsum_ready, LAYERS + 1)
            for k in range(KC):
                ins = mm(bank[5][:, k:k + 1], hsum[:, k * P:(k + 1) * P], mean_w[:, 0:1], start=True, stop=True)
            ins.then_inc(xmean_done, 1)
            pe.wait_ge(xmean_copied, 1)
            for k in range(KC):
                ins = mm(bank[5][0:1, 0:EX], mcol[:, k:k + 1], Wr_s[:, k, :], start=k == 0, stop=k == KC - 1)
            ins.then_inc(logits_done, 1)
            pe.wait_ge(w_ready, 1)
            mm(bank[5][:, 0:TOP], ones[0:1, :], ra[:, 9, 0:TOP], start=True, stop=True).then_inc(w_spread, 1)

            def turn(t, u, r):
                pe.wait_ge(xf_ready, t + 1)
                if u >= 2:
                    pe.wait_ge(xfT_copied, t - 1)
                for k in range(KC):
                    ins = nc.tensor.transpose(T3[3 + u % 2][:, k, 0:r], U[0:r, u, k * P:(k + 1) * P], ident[0:r, 0:r])
                ins.then_inc(xfT_done, 1)

            def up(s, g0, ntile, w):
                pe.wait_ge(xfT_copied, ntile)
                for f in range(TOP * FC):
                    if f >= 3:
                        pe.wait_ge(gelu_done, g0 + f - 2)
                    for k in range(KC):
                        ins = mm(bank[f % 3][:, 0:w], W1_s[:, f // FC * KC + k, f % FC:FF:FC], xfT[:, k, 0:w],
                                 start=k == 0, stop=k == KC - 1)
                    ins.then_inc(up_done, 1)

            def down(g0, u, r):
                for f in range(TOP * FC):
                    ins = mm(bank[5 + u][0:r, 0:D], gT[:, f, u * P:u * P + r], W2_s[:, f // FC, f % FC, :],
                             start=f == 0, stop=f == TOP * FC - 1)
                ins.then_inc(down_done, 1)
            F8 = TOP * FC
            for u in range(SUP):
                turn(u, u, P)
            pe.wait_ge(w1_in, 16 * 2 * TOP)
            with pe.Fori(0, LOOP - 1) as i:
                up(i, i * F8, (i + 1) * SUP, SUP * P)
                for u in range(SUP):
                    turn((i + 1) * SUP + u, u, P)
                pe.wait_ge(gelu_done, (i + 1) * F8)
                pe.wait_ge(ew_ready, 1)
                for u in range(SUP):
                    pe.wait_ge(out_ready, (i + 1) * SUP)
                    down(i * F8, u, P)
            up(LOOP - 1, (LOOP - 1) * F8, T - 1, SUP * P)
            turn(T - 1, 0, LAST)
            pe.wait_ge(gelu_done, LOOP * F8)
            for u in range(SUP):
                pe.wait_ge(out_ready, T - 1)
                down((LOOP - 1) * F8, u, P)
            up(LOOP, LOOP * F8, T, LAST)
            pe.wait_ge(gelu_done, (LOOP + 1) * F8)
            pe.wait_ge(out_ready, T)
            down(LOOP * F8, 0, LAST)


WTS = 16 * (2 + 4 * LAYERS + 1 + 4)

_INS = ["x", "src", "dst", "L0_gnn_W_in", "L0_gnn_b_in", "L0_gnn_Wl", "L0_gnn_bl", "L0_gnn_Wg", "L0_gnn_bg",
        "L0_gnn_gamma", "L0_gnn_beta", "L0_ffn_Wr", "L0_ffn_br", "L0_ffn_W1", "L0_ffn_b1", "L0_ffn_W2", "L0_ffn_b2",
        "L0_ffn_gamma", "L0_ffn_beta"]


def kernel(**inputs):
    import numpy as np
    import concourse.bacc as bacc
    from concourse.bass_utils import run_bass_kernel_spmd

    nc = bacc.Bacc("TRN2", target_bir_lowering=False, num_devices=1)
    arrays, args = {}, []
    for name in _INS:
        a = np.ascontiguousarray(inputs[name])
        arrays[f"in_{name}"] = a
        args.append(nc.dram_tensor(f"in_{name}", a.shape, mybir.dt.from_np(a.dtype), kind="ExternalInput").ap())
    out = nc.dram_tensor("out", [N, D], F32, kind="ExternalOutput").ap()
    build(nc, *args, out)
    r = run_bass_kernel_spmd(nc, [arrays], core_ids=[0])
    return r.results[0]["out"]
```
